# Optimizing a Trainium2 kernel written in Bass

```python
import numpy as np
import jax
import jax.numpy as jnp

def _softmax(x, axis=-1):
    return jax.nn.softmax(x, axis=axis)

def _gelu(x):
    return jax.nn.gelu(x, approximate=True)

def _silu(x):
    return jax.nn.silu(x)

def _sigmoid(x):
    return jax.nn.sigmoid(x)

def _layernorm(x, axis=-1, eps=1e-05):
    m = jnp.mean(x, axis=axis, keepdims=True)
    v = jnp.var(x, axis=axis, keepdims=True)
    return (x - m) / jnp.sqrt(v + eps)

def _scatter_add(tgt, idx, src, axis=0):
    return tgt.at[idx].add(src)

def _segment_sum(src, seg, n):
    return jax.ops.segment_sum(src, seg, n)
kernel_name = 'mk_xattn_ffn_d2_seqx_r8_62f09e'

def setup_inputs(seed: int=0):
    np.random.seed(seed)
    _w = jnp.asarray

    def _rec_inputs():
        import jax
        import jax.numpy as jnp
        _rk = jax.random.key(seed)
        x = 0.0001212 + 1 * jax.random.normal(jax.random.fold_in(_rk, 1), (16, 128, 256), jnp.float32)
        _lenS = 128 - jax.random.randint(jax.random.fold_in(_rk, 7), (16,), 0, max(1, 128 // 4) + 1, jnp.int32)
        _lenS2 = 128 - jax.random.randint(jax.random.fold_in(_rk, 8), (16,), 0, max(1, 128 // 4) + 1, jnp.int32)
        _ctx_2048P = jax.random.normal(jax.random.fold_in(_rk, 11), (16, 16, 256), jnp.float32)
        _ctx_2048c = jax.random.dirichlet(jax.random.fold_in(_rk, 511), 0.3 * jnp.ones((16,), jnp.float32), (16, 128))
        _ctx_2048t = jnp.einsum('bsk,bkd->bsd', _ctx_2048c, _ctx_2048P)
        _ctx_2048t = _ctx_2048t * jax.lax.rsqrt(jnp.mean(jnp.square(_ctx_2048t)) + 1e-12) * 0.953939
        ctx_2048 = 0.000173663 + 1.0001 * (_ctx_2048t + 0.3 * jax.random.normal(jax.random.fold_in(_rk, 611), (16, 128, 256), jnp.float32))
        return (x, ctx_2048)
    x, ctx_2048 = _rec_inputs()

    def _L0_xattn_setup():
        import jax, jax.numpy as jnp
        import numpy as np
        B_DIM, T_DIM, C_DIM = (16, 128, 256)

        def _wkv(w, u, k, v):
            Bn, Tn, Cn = k.shape
            NEG_INF = jnp.float32(-1e+38)

            def step(carry, kv_t):
                p, q, o = carry
                kt, vt = kv_t
                no = jnp.maximum(o, u + kt)
                A = jnp.exp(o - no)
                E = jnp.exp(u + kt - no)
                y = (A * p + E * vt) / (A * q + E)
                no2 = jnp.maximum(w + o, kt)
                A2 = jnp.exp(w + o - no2)
                E2 = jnp.exp(kt - no2)
                return ((A2 * p + E2 * vt, A2 * q + E2, no2), y)
            init = (jnp.zeros((Bn, Cn), k.dtype), jnp.zeros((Bn, Cn), k.dtype), jnp.full((Bn, Cn), NEG_INF, k.dtype))
            kT = jnp.moveaxis(k, 1, 0)
            vT = jnp.moveaxis(v, 1, 0)
            _, yT = jax.lax.scan(step, init, (kT, vT))
            return jnp.moveaxis(yT, 0, 1)
        key = jax.random.key(seed)
        k1, k2, k3, k4 = jax.random.split(key, 4)
        w = -jnp.exp(jax.random.normal(k1, (C_DIM,), jnp.float32))
        u = jax.random.normal(k2, (C_DIM,), jnp.float32)
        k = jax.random.normal(k3, (B_DIM, T_DIM, C_DIM), jnp.float32)
        v = jax.random.normal(k4, (B_DIM, T_DIM, C_DIM), jnp.float32)
        return {'B': B_DIM, 'T': T_DIM, 'C': C_DIM, 'w': w, 'u': u, 'k': k, 'v': v}
    _L0_xattn_all = _L0_xattn_setup()
    _L0_xattn_in = {k: v for k, v in _L0_xattn_all.items() if k in ('w', 'u')}
    del _L0_xattn_all

    def _L0_ffn_setup():
        import jax, jax.numpy as jnp
        import numpy as np
        from jax import lax
        H = 256
        I = 176
        E = 16
        TOP_K = 6
        IS = 2 * I

        def _swiglu(x, w13_, w2_):
            gu = x @ w13_.T
            g, u = jnp.split(gu, 2, axis=-1)
            return jax.nn.silu(g) * u @ w2_.T
        key = jax.random.key(seed)
        ks = jax.random.split(key, 6)
        return {'hidden_states': jax.random.normal(ks[0], (1, 256, H), jnp.float32), 'gate_w': jax.random.normal(ks[1], (E, H), jnp.float32) * 0.02, 'w13': jax.random.normal(ks[2], (E, 2 * I, H), jnp.float32) * 0.02, 'w2': jax.random.normal(ks[3], (E, H, I), jnp.float32) * 0.02, 'sw13': jax.random.normal(ks[4], (2 * IS, H), jnp.float32) * 0.02, 'sw2': jax.random.normal(ks[5], (H, IS), jnp.float32) * 0.02}
    _L0_ffn_all = _L0_ffn_setup()
    _L0_ffn_in = {k: v for k, v in _L0_ffn_all.items() if k in ('gate_w', 'w13', 'w2', 'sw13', 'sw2')}
    del _L0_ffn_all

    def _L1_xattn_setup():
        import jax, jax.numpy as jnp
        import numpy as np
        import math
        N_HEADS = 8
        key = jax.random.key(seed)
        k1, k2, k3 = jax.random.split(key, 3)
        N, W, T, S = (4, 64, 256, 256)
        q = jax.random.normal(k1, (N, W, T), dtype=jnp.float32)
        k = jax.random.normal(k2, (N, W, S), dtype=jnp.float32)
        v = jax.random.normal(k3, (N, W, S), dtype=jnp.float32)
        return {'q': q, 'k': k, 'v': v}
    _L1_xattn_all = _L1_xattn_setup()
    _L1_xattn_in = {k: v for k, v in _L1_xattn_all.items() if k in ()}
    del _L1_xattn_all

    def _L1_ffn_setup():
        import jax, jax.numpy as jnp
        import numpy as np
        EPS = 1e-07
        CURVATURE = 1.0
        MAX_NORM_RATIO = 0.99
        B, L, N, K = (4, 256, 256, 256)

        def _ternary_init(key, n, k):
            rand = jax.random.normal(key, (n, k), dtype=jnp.float32)
            threshold = 0.5 * jnp.mean(jnp.abs(rand))
            return jnp.where(rand > threshold, 1.0, jnp.where(rand < -threshold, -1.0, 0.0)).astype(jnp.float32)
        key = jax.random.key(seed)
        kx, kw = jax.random.split(key)
        x = jax.random.normal(kx, (B, L, N), dtype=jnp.float32)
        weight = _ternary_init(kw, N, K)
        scale = jnp.full((K,), 1.0 / np.sqrt(N), dtype=jnp.float32)
        return {'x': x, 'weight': weight, 'scale': scale}
    _L1_ffn_all = _L1_ffn_setup()
    _L1_ffn_in = {k: v for k, v in _L1_ffn_all.items() if k in ('weight', 'scale')}
    del _L1_ffn_all
    return {'x': x, 'ctx_2048': ctx_2048, 'L0_xattn_w': _L0_xattn_in['w'], 'L0_xattn_u': _L0_xattn_in['u'], 'L0_ffn_gate_w': _L0_ffn_in['gate_w'], 'L0_ffn_w13': _L0_ffn_in['w13'], 'L0_ffn_w2': _L0_ffn_in['w2'], 'L0_ffn_sw13': _L0_ffn_in['sw13'], 'L0_ffn_sw2': _L0_ffn_in['sw2'], 'L1_ffn_weight': _L1_ffn_in['weight'], 'L1_ffn_scale': _L1_ffn_in['scale']}

def reference(x, ctx_2048, L0_xattn_w, L0_xattn_u, L0_ffn_gate_w, L0_ffn_w13, L0_ffn_w2, L0_ffn_sw13, L0_ffn_sw2, L1_ffn_weight, L1_ffn_scale):
    import jax
    import jax.numpy as jnp

    def _L0_xattn_ref(B, T, C, w, u, k, v):
        import jax, jax.numpy as jnp
        import numpy as np
        B_DIM, T_DIM, C_DIM = (16, 128, 256)

        def _wkv(w, u, k, v):
            Bn, Tn, Cn = k.shape
            NEG_INF = jnp.float32(-1e+38)

            def step(carry, kv_t):
                p, q, o = carry
                kt, vt = kv_t
                no = jnp.maximum(o, u + kt)
                A = jnp.exp(o - no)
                E = jnp.exp(u + kt - no)
                y = (A * p + E * vt) / (A * q + E)
                no2 = jnp.maximum(w + o, kt)
                A2 = jnp.exp(w + o - no2)
                E2 = jnp.exp(kt - no2)
                return ((A2 * p + E2 * vt, A2 * q + E2, no2), y)
            init = (jnp.zeros((Bn, Cn), k.dtype), jnp.zeros((Bn, Cn), k.dtype), jnp.full((Bn, Cn), NEG_INF, k.dtype))
            kT = jnp.moveaxis(k, 1, 0)
            vT = jnp.moveaxis(v, 1, 0)
            _, yT = jax.lax.scan(step, init, (kT, vT))
            return jnp.moveaxis(yT, 0, 1)
        return _wkv(w, u, k, v)

    def _L0_ffn_ref(hidden_states, gate_w, w13, w2, sw13, sw2):
        import jax, jax.numpy as jnp
        import numpy as np
        from jax import lax
        H = 256
        I = 176
        E = 16
        TOP_K = 6
        IS = 2 * I

        def _swiglu(x, w13_, w2_):
            gu = x @ w13_.T
            g, u = jnp.split(gu, 2, axis=-1)
            return jax.nn.silu(g) * u @ w2_.T
        B, S, Hd = hidden_states.shape
        x = hidden_states.reshape(-1, Hd)
        T = x.shape[0]
        scores = jax.nn.softmax(x @ gate_w.T, axis=-1)
        topk_w, topk_ids = lax.top_k(scores, TOP_K)
        topk_w = topk_w / (topk_w.sum(-1, keepdims=True) + 1e-20)
        combine = jnp.einsum('tk,tke->te', topk_w, jax.nn.one_hot(topk_ids, E, dtype=topk_w.dtype))

        def body(acc, ew):
            w13_e, w2_e, c_e = ew
            y = _swiglu(x, w13_e, w2_e)
            return (acc + c_e[:, None] * y, None)
        out, _ = lax.scan(body, jnp.zeros_like(x), (w13, w2, combine.T))
        out = out + _swiglu(x, sw13, sw2)
        return out.reshape(B, S, Hd)

    def _L1_xattn_ref(q, k, v):
        import jax, jax.numpy as jnp
        import numpy as np
        import math
        N_HEADS = 8
        bs, width, T = q.shape
        S = k.shape[-1]
        ch = width // N_HEADS
        qh = q.reshape(bs * N_HEADS, ch, T)
        kh = k.reshape(bs * N_HEADS, ch, S)
        vh = v.reshape(bs * N_HEADS, ch, S)
        scale = 1.0 / math.sqrt(ch)
        attn = jnp.einsum('bct,bcs->bts', qh * scale, kh * scale)
        attn = jax.nn.softmax(attn, axis=-1)
        out = jnp.einsum('bts,bcs->bct', attn, vh)
        return out.reshape(bs, width, T)

    def _L1_ffn_ref(x, weight, scale):
        import jax, jax.numpy as jnp
        import numpy as np
        EPS = 1e-07
        CURVATURE = 1.0
        MAX_NORM_RATIO = 0.99
        B, L, N, K = (4, 256, 256, 256)

        def _ternary_init(key, n, k):
            rand = jax.random.normal(key, (n, k), dtype=jnp.float32)
            threshold = 0.5 * jnp.mean(jnp.abs(rand))
            return jnp.where(rand > threshold, 1.0, jnp.where(rand < -threshold, -1.0, 0.0)).astype(jnp.float32)
        sqrt_c = jnp.sqrt(jnp.float32(CURVATURE))
        out = jnp.einsum('bln,nk->blk', x, weight) * scale
        v_norm = jnp.maximum(jnp.linalg.norm(out, axis=-1, keepdims=True), EPS)
        scaled_norm = sqrt_c * v_norm
        out = out * (jnp.tanh(scaled_norm) / (scaled_norm + EPS))
        max_norm = MAX_NORM_RATIO / sqrt_c
        o_norm = jnp.maximum(jnp.linalg.norm(out, axis=-1, keepdims=True), EPS)
        out = out * jnp.minimum(max_norm / o_norm, 1.0)
        return out.astype(x.dtype)
    x = x + _L0_xattn_ref(16, 128, 256, L0_xattn_w, L0_xattn_u, _layernorm(x, axis=-1), ctx_2048)
    x = x + _L0_ffn_ref(_layernorm(x, axis=-1), L0_ffn_gate_w, L0_ffn_w13, L0_ffn_w2, L0_ffn_sw13, L0_ffn_sw2)
    x = x + _L1_xattn_ref(_layernorm(x, axis=-1), ctx_2048, ctx_2048)
    x = x + _L1_ffn_ref(_layernorm(x, axis=-1), L1_ffn_weight, L1_ffn_scale)
    return x

_drawn_inputs = setup_inputs


def setup_inputs(seed=0):
    import zlib

    import numpy as np

    out = dict(_drawn_inputs(seed))
    spreads = {'L1_ffn_scale': (0.0625, 0.6)}
    factors = {'L0_ffn_gate_w': 8.0,
     'L0_ffn_w13': 8.0,
     'L0_ffn_w2': 8.0,
     'L0_ffn_sw13': 3.668,
     'L0_ffn_sw2': 3.67}
    for name, (base, spread) in spreads.items():
        noise = np.random.default_rng([zlib.crc32(name.encode()), seed]).standard_normal(out[name].shape)
        drawn = base * np.exp(spread * noise) if base else spread * noise
        out[name] = jnp.asarray(drawn.astype(out[name].dtype))
    for name, factor in factors.items():
        out[name] = (out[name] * factor).astype(out[name].dtype)
    return out
```

```python
from contextlib import ExitStack

import concourse.bass as bass
from concourse import mybir

F32 = mybir.dt.float32
F32R = mybir.dt.float32r
F16 = mybir.dt.float16
BF16 = mybir.dt.bfloat16
ALU = mybir.AluOpType
ACT = mybir.ActivationFunctionType
AX_X = mybir.AxisListType.X

P = 128
BATCH, POS, FEAT = 16, 128, 256
HALF = FEAT // P
BB = 4
BLOCKS = BATCH // BB
TOK = BB * POS
EXPERTS, INNER, TOP_K = 16, 176, 6
SHARED = 2 * INNER
TILES = -(-(EXPERTS * INNER + SHARED) // P)
HEADS = 8
CH = POS // HEADS
PAIRS = HEADS // 2
STACK = 6 * CH
LN_EPS = 1e-5
BALL_EPS = 1e-7
MAX_NORM = 0.99
NEG = -1e38
BF16_ONE = 0x3F80
CLAMP = 60.0

W_SCALE = 64.0
H_SCALE = 8.0
ROUTE_SCALE = H_SCALE * 0.5 / (W_SCALE * W_SCALE)

SLOTS = 3 * TILES
WKV_START = 23 - SLOTS
WKV_HALF = 13
ATTN_GAP = 18
FIRST_SLOT = WKV_START
ATTN_LAST = 38
LAST_SLOT = SLOTS * BLOCKS + 5 + ATTN_GAP * (BB - 1) + ATTN_LAST


def wkv_start(n):
    return WKV_START + SLOTS * n


def attn_start(m):
    return SLOTS * (m // BB + 1) + 5 + ATTN_GAP * (m % BB)


def attn_steps(slot):
    return [(m, slot - attn_start(m)) for m in range(BATCH) if 0 <= slot - attn_start(m) <= ATTN_LAST]


def wkv_steps(slot):
    return [(n, slot - wkv_start(n)) for n in range(BLOCKS) if 0 <= slot - wkv_start(n) < SLOTS]


def bank_uses():
    misc, score = {}, {}
    for slot in range(FIRST_SLOT, LAST_SLOT + 1):
        for m, a in attn_steps(slot):
            if 6 <= a < 14:
                score[("max", m, a - 6)] = len(score) + 1
            if a == 14:
                misc[("shift", m)] = len(misc) + 1
            if 18 <= a < 26:
                score[("exp", m, a - 18)] = len(score) + 1
            if a == 28:
                misc[("sums", m)] = len(misc) + 1
            if a == 32:
                misc[("x4", m)] = len(misc) + 1
            if a == 33:
                misc[("ffn", m)] = len(misc) + 1
        for n, w in wkv_steps(slot):
            for h in range(HALF):
                if w == 3 + h:
                    misc[("k", n, h)] = len(misc) + 1
                if w == 16 + WKV_HALF * h:
                    misc[("y", n, h)] = len(misc) + 1
                if w == 33 + 2 * h:
                    misc[("x2", n, h)] = len(misc) + 1
            if w == 38:
                misc[("gate", n)] = len(misc) + 1
            if w == 46:
                misc[("route", n)] = len(misc) + 1
    return misc, score


def build(nc, x, ctx_feat, ctx_heads, experts, gate_w, decay_bonus, ffn_w, ffn_scale, rows_of, sums_of, eye, eye_b, out):
    misc_no, score_no = bank_uses()
    q_scratch = nc.dram_tensor("q_scratch", (2, 2, P, FEAT), F32, kind="Internal").ap()
    m_scratch = nc.dram_tensor("m_scratch", (2, HEADS, FEAT), F32, kind="Internal").ap()

    with ExitStack() as ctx:
        def sb(name, shape, dt=F32):
            return ctx.enter_context(nc.sbuf_tensor(name, shape, dt))

        def bank(name):
            return ctx.enter_context(nc.psum_tensor(name, [P, 512], F32))

        w13_hi = sb("w13_hi", [P, TILES, 2, HALF, P], F16)
        w13_lo = sb("w13_lo", [P, TILES, 2, HALF, P], F16)
        w2_hi = sb("w2_hi", [P, TILES, FEAT], F16)
        w2_lo = sb("w2_lo", [P, TILES, FEAT], F16)
        gw = sb("gw", [P, HALF, EXPERTS])
        gw_hi = sb("gw_hi", [P, HALF, EXPERTS], F16)
        gw_lo = sb("gw_lo", [P, HALF, EXPERTS], F16)
        arena = sb("arena", [P, 9 * FEAT])
        stage = [arena[:, 3 * FEAT * i:3 * FEAT * (i + 1)] for i in range(3)]
        ysb = arena[:, 0:HALF * TOK].rearrange("p (h t) -> p h t", h=HALF)
        kraw = arena[0:STACK, 4 * FEAT:8 * FEAT].rearrange("p (a k) -> p a k", a=PAIRS)
        vb = arena[:, 8 * FEAT:9 * FEAT].rearrange("p (h t) -> p h t", h=HALF)
        rows_sb = sb("rows_sb", [96, TILES * P], BF16)
        sums_sb = sb("sums_sb", [P, P])
        eye_sb = sb("eye_sb", [P, P])
        eye_b_sb = sb("eye_b_sb", [P, P], BF16)
        wu = sb("wu", [P, HALF, 2])
        ffn_sb = sb("ffn_sb", [P, HALF, FEAT])
        ffn_s = sb("ffn_s", [P, FEAT])
        neg_half = sb("neg_half", [P, BB])
        pos_half = sb("pos_half", [P, 1])
        res = [sb(f"res{i}", [P, BB, FEAT]) for i in range(3)]
        xn = sb("xn", [P, BB, FEAT])
        vT = sb("vT", [P, HALF, BB, POS])
        kT = [sb(f"kT{h}", [P, BB, POS]) for h in range(HALF)]
        top = sb("top", [P, BB, POS + 1])
        num_s = sb("num_s", [P, BB, POS + 1])
        den_s = sb("den_s", [P, BB, POS + 1])
        keep = sb("keep", [P, BB, POS])
        take = sb("take", [P, BB, POS])
        now = sb("now", [P, BB, POS])
        take_v = sb("take_v", [P, BB, POS])
        now_v = sb("now_v", [P, BB, POS])
        yk = take_v
        stats = sb("stats", [P, BB, 6])
        mv = sb("mv", [P, BB, 2])
        ve = sb("ve", [P, BB])
        rstd = sb("rstd", [P, BB])
        lg = sb("lg", [P, BB, EXPERTS])
        lmax = sb("lmax", [P, BB])
        ex = sb("ex", [P, BB, EXPERTS])
        small = sb("small", [P, 4, BB])
        probs = sb("probs", [P, BB, EXPERTS + 2])
        top8 = sb("top8", [P, BB, 8])
        rest = sb("rest", [P, BB, EXPERTS + 2])
        route = sb("route", [P, BB, EXPERTS])
        route3 = sb("route3", [P, BB, 96], BF16)
        cT = [sb(f"cT{i}", [96, TOK], BF16) for i in range(2)]
        xT_hi = [sb(f"xT_hi{i}", [P, HALF, TOK], F16) for i in range(2)]
        xT_lo = [sb(f"xT_lo{i}", [P, HALF, TOK], F16) for i in range(2)]
        th = sb("th", [P, TOK])
        t1 = sb("t1", [P, TOK])
        hb = [sb(f"hb{i}", [P, TOK]) for i in range(2)]
        h_hi = [sb(f"h_hi{i}", [P, TOK], F16) for i in range(2)]
        h_lo = [sb(f"h_lo{i}", [P, TOK], F16) for i in range(2)]
        stats3 = sb("stats3", [P, 6])
        mv3 = sb("mv3", [P, 2])
        ve3 = sb("ve3", [P, 1])
        rstd3 = sb("rstd3", [P, 1])
        q = sb("q", [P, FEAT])
        q_hi = sb("q_hi", [P, FEAT], F32R)
        q_lo = sb("q_lo", [P, FEAT], F32R)
        qz = [sb(f"qz{i}", [P, PAIRS, 2 * FEAT], F32R) for i in range(2)]
        ks = [sb(f"ks{i}", [P, PAIRS, FEAT], F32R) for i in range(2)]
        vz = sb("vz", [P, HALF, HEADS * (P + CH)])
        mx = sb("mx", [P, HALF, HEADS])
        shift = sb("shift", [HEADS, FEAT], F32R)
        pr = [sb(f"pr{i}", [P, 2 * FEAT]) for i in range(2)]
        sums = sb("sums", [P, FEAT])
        rsum = sb("rsum", [P, FEAT])
        stats4 = sb("stats4", [P, 6])
        mv4 = sb("mv4", [P, 2])
        ve4 = sb("ve4", [P, 1])
        rstd4 = sb("rstd4", [P, 1])
        x4n = sb("x4n", [P, FEAT])
        x4T = sb("x4T", [P, HALF, POS])
        fo = sb("fo", [P, FEAT])
        sc = sb("sc", [P, 12])

        gate_ps, up_ps, route_ps = bank("gate_ps"), bank("up_ps"), bank("route_ps")
        y_ps = [bank("y_ps0"), bank("y_ps1")]
        score_ps, av_ps, misc_ps = bank("score_ps"), bank("av_ps"), bank("misc_ps")
        misc_b = misc_ps[:, :].bitcast(BF16)

        def sem(name):
            return ctx.enter_context(nc.semaphore(name))

        early_in = sem("early_in")
        consts_in = sem("consts_in")
        consts_set = sem("consts_set")
        gate_w_hi = sem("gate_w_hi")
        gate_w_lo = sem("gate_w_lo")
        x_in = sem("x_in")
        v_in = sem("v_in")
        var_ready = sem("var_ready")
        rstd_ready = sem("rstd_ready")
        xn_ready = sem("xn_ready")
        top_ready = sem("top_ready")
        own_ready = sem("own_ready")
        gaps_ready = sem("gaps_ready")
        exps_ready = sem("exps_ready")
        vs_ready = sem("vs_ready")
        yk_ready = sem("yk_ready")
        x2_hi_ready = sem("x2_hi_ready")
        dve_step = sem("dve_step")
        logits_exp = sem("logits_exp")
        split_ready = sem("split_ready")
        w13_hi_ready = sem("w13_hi_ready")
        w13_lo_ready = sem("w13_lo_ready")
        w2_hi_ready = sem("w2_hi_ready")
        w2_lo_ready = sem("w2_lo_ready")
        gate_ready = sem("gate_ready")
        tanh_ready = sem("tanh_ready")
        gate_used = sem("gate_used")
        route_ready = sem("route_ready")
        route_used = sem("route_used")
        up_ready = sem("up_ready")
        h_ready = sem("h_ready")
        h_hi_ready = sem("h_hi_ready")
        h_lo_ready = sem("h_lo_ready")
        y_done = sem("y_done")
        y_copied = sem("y_copied")
        y_turned = sem("y_turned")
        y_added = sem("y_added")
        var3_ready = sem("var3_ready")
        rstd3_ready = sem("rstd3_ready")
        q_ready = sem("q_ready")
        q_hi_ready = sem("q_hi_ready")
        q_lo_ready = sem("q_lo_ready")
        kraw_in = sem("kraw_in")
        ks_hi_ready = sem("ks_hi_ready")
        ks_ready = sem("ks_ready")
        vb_in = sem("vb_in")
        vz_ready = sem("vz_ready")
        q_out0 = sem("q_out0")
        q_out1 = sem("q_out1")
        qz_in0 = sem("qz_in0")
        qz_in1 = sem("qz_in1")
        shift_out = sem("shift_out")
        shift_in = sem("shift_in")
        score_written = sem("score_written")
        score_read = sem("score_read")
        av_done = sem("av_done")
        sums_set = sem("sums_set")
        av_read = sem("av_read")
        var4_ready = sem("var4_ready")
        rstd4_ready = sem("rstd4_ready")
        x4_ready = sem("x4_ready")
        misc_written = sem("misc_written")
        misc_read = sem("misc_read")
        square_ready = sem("square_ready")
        norm_ready = sem("norm_ready")
        norm1_ready = sem("norm1_ready")
        tanh1_ready = sem("tanh1_ready")
        res_ready = sem("res_ready")
        stored = sem("stored")
        stage_in = [sem(f"stage_in{i}") for i in range(3)]
        q_out = [q_out0, q_out1]
        qz_in = [qz_in0, qz_in1]

        N_EARLY = 3
        N_CONSTS = 5
        N_SET = 16

        def heads_view(flat, st, h):
            return flat[:, st, h * P:(h + 1) * P]

        block = ctx.enter_context(nc.Block())

        @block.sync
        def _(sp):
            def load_const(dst, src):
                sp.dma_start(dst, src).then_inc(consts_in, 16)

            sp.dma_start(wu[:, :, :], decay_bonus).then_inc(early_in, 16)
            sp.dma_start(eye_sb[:, :], eye).then_inc(early_in, 16)
            sp.dma_start(gw[:, :, :], gate_w).then_inc(early_in, 16)

            def wkv(n, w):
                if w != 0:
                    return
                if n >= 3:
                    sp.wait_ge(stored, 16 * BB * (n - 2))
                sp.dma_start(res[n % 3][:, :, :], x[BB * n:BB * n + BB].rearrange("b t c -> t b c")).then_inc(x_in, 16)
                if n >= 3:
                    sp.wait_ge(x_in, 16 * (n - 2))
                if n >= 1:
                    sp.wait_ge(v_in, 32 * n)
                    sp.wait_ge(vs_ready, 4 * n)
                for h in range(HALF):
                    sp.dma_start(vT[:, h, :, :], ctx_feat[BB * n:BB * n + BB, h * P:(h + 1) * P, :].rearrange("b p t -> p b t")).then_inc(v_in, 16)
                if n == 0:
                    load_const(eye_b_sb[:, :], eye_b.bitcast(BF16))
                    load_const(rows_sb[:, :], rows_of.bitcast(BF16))
                    load_const(sums_sb[:, :], sums_of)
                    load_const(ffn_sb[:, :, :], ffn_w)
                    load_const(ffn_s[:, :], ffn_scale.partition_broadcast(P))

            def weights(slot):
                if slot % 3 == 0 and 0 <= slot // 3 + 5 < TILES:
                    j = slot // 3 + 5
                    if j >= 3:
                        sp.wait_ge(w13_hi_ready, j - 2)
                        sp.wait_ge(w13_lo_ready, j - 2)
                        sp.wait_ge(w2_lo_ready, j - 2)
                        sp.wait_ge(stage_in[j % 3], 16 * (j // 3))
                    sp.dma_start(stage[j % 3], experts[j]).then_inc(stage_in[j % 3], 16)

            def attention(m, a):
                i = m % 2
                if a == 0:
                    if m >= 1:
                        sp.wait_ge(ks_ready, m)
                        sp.wait_ge(vz_ready, m)
                        sp.wait_ge(kraw_in, 16 * m)
                        sp.wait_ge(vb_in, 16 * m)
                    else:
                        sp.wait_ge(w2_lo_ready, TILES)
                        for i in range(3):
                            sp.wait_ge(stage_in[i], 16 * len(range(i, TILES, 3)))
                    sp.dma_start(kraw, ctx_heads[m]).then_inc(kraw_in, 16)
                    sp.dma_start(vb, ctx_feat[m].rearrange("(h p) t -> p h t", p=P)).then_inc(vb_in, 16)
                if a == 2:
                    sp.wait_ge(q_hi_ready, m + 1)
                    if m >= 2:
                        sp.wait_ge(qz_in[i], 96 * (m // 2))
                    sp.dma_start(q_scratch[i, 0], q_hi[:, :].bitcast(F32)).then_inc(q_out[i], 16)
                    sp.wait_ge(q_lo_ready, m + 1)
                    sp.dma_start(q_scratch[i, 1], q_lo[:, :].bitcast(F32)).then_inc(q_out[i], 16)
                if a == 4:
                    sp.wait_ge(q_out[i], 32 * (m // 2 + 1))
                    if m >= 2:
                        sp.wait_ge(score_written, score_no[("exp", m - 2, 7)])
                    for row, part, head, col in ((0, 0, 0, 0), (16, 1, 0, 0), (64, 0, 0, 0),
                                                 (32, 0, 4, FEAT), (48, 1, 4, FEAT), (80, 0, 4, FEAT)):
                        src = q_scratch[i, part, head * CH:(head + PAIRS) * CH, :].rearrange("(p c) t -> c p t", c=CH)
                        sp.dma_start(qz[i][row:row + CH, :, col:col + FEAT].bitcast(F32), src).then_inc(qz_in[i], 16)
                if a == 15:
                    sp.wait_ge(misc_read, misc_no[("shift", m)])
                    if m >= 2:
                        sp.wait_ge(shift_in, 32 * (m - 1))
                    sp.dma_start(m_scratch[i], shift[:, :].bitcast(F32)).then_inc(shift_out, 16)
                    sp.wait_ge(shift_out, 16 * (m + 1))
                    for half in range(2):
                        sp.dma_start(qz[i][STACK + half:STACK + half + 1, :, half * FEAT:(half + 1) * FEAT].bitcast(F32),
                                     m_scratch[i:i + 1, half * PAIRS:(half + 1) * PAIRS, :]).then_inc(shift_in, 16)
                if a == ATTN_LAST:
                    sp.wait_ge(res_ready, m + 1)
                    sp.dma_start(out[m], res[(m // BB) % 3][:, m % BB, :]).then_inc(stored, 16)

            for slot in range(FIRST_SLOT, LAST_SLOT + 1):
                weights(slot)
                for m, a in attn_steps(slot):
                    attention(m, a)
                for n, w in wkv_steps(slot):
                    wkv(n, w)
            sp.wait_ge(stored, 16 * BATCH)

        @block.gpsimd
        def _(pool):
            nc.gpsimd.memset(neg_half[:, :], -0.5).then_inc(consts_set, 1)
            nc.gpsimd.memset(pos_half[:, :], 0.5).then_inc(consts_set, 1)
            nc.gpsimd.memset(top[:, :, 0:1], NEG).then_inc(consts_set, 1)
            nc.gpsimd.memset(num_s[:, :, 0:1], 0.0).then_inc(consts_set, 1)
            nc.gpsimd.memset(den_s[:, :, 0:1], 0.0).then_inc(consts_set, 1)
            nc.gpsimd.memset(probs[:, :, EXPERTS:EXPERTS + 2], 3.0).then_inc(consts_set, 1)
            nc.gpsimd.memset(route3[:, :, :], 0.0).then_inc(consts_set, 1)
            nc.gpsimd.memset(sums[:, :], 0.0).then_inc(consts_set, 1)
            nc.gpsimd.memset(vz[:, :, :], 0.0).then_inc(consts_set, 1)
            for i in range(2):
                nc.gpsimd.memset(qz[i][:, :, :].bitcast(F32), 0.0).then_inc(consts_set, 1)
            pool.wait_ge(consts_set, 13)
            nc.gpsimd.memset(route3[:, :, EXPERTS:EXPERTS + 1], ROUTE_SCALE).then_inc(consts_set, 1)
            for h in range(HEADS):
                col = h * P + (96 + h if h < PAIRS else h - PAIRS)
                ins = nc.gpsimd.memset(vz[:, :, col:col + 1], 1.0)
                if h >= HEADS - 2:
                    ins.then_inc(consts_set, 1)

            def norm_scale(var_ready, no, dst, src, width, rstd_ready):
                pool.wait_ge(var_ready, no)
                nc.gpsimd.tensor_tensor(dst, src, neg_half[:, 0:width], ALU.pow).then_inc(rstd_ready, 1)

            def moe(slot):
                t, r = slot // 3, slot % 3
                if r == 2 and 0 <= t < TILES * BLOCKS:
                    pool.wait_ge(h_hi_ready, t + 1)
                    nc.gpsimd.tensor_tensor(h_lo[t % 2][:, :], hb[t % 2][:, :], h_hi[t % 2][:, :],
                                            ALU.subtract).then_inc(h_lo_ready, 1)

            def weights(slot):
                if slot % 3 == 0 and 0 <= slot // 3 + 3 < TILES:
                    j = slot // 3 + 3
                    pool.wait_ge(w2_hi_ready, j + 1)
                    pool.wait_ge(w13_lo_ready, j + 1)
                    nc.gpsimd.tensor_tensor(w2_lo[:, j, :], stage[j % 3][:, 2 * FEAT:3 * FEAT], w2_hi[:, j, :],
                                            ALU.subtract).then_inc(w2_lo_ready, 1)

            def attention(m, a):
                i = m % 2
                if a == 0:
                    norm_scale(var3_ready, m + 1, rstd3[:, :], ve3[:, :], 1, rstd3_ready)
                if a == 1:
                    pool.wait_ge(q_hi_ready, m + 1)
                    if m >= 1:
                        pool.wait_ge(q_out[(m - 1) % 2], 32 * ((m - 1) // 2 + 1))
                    nc.gpsimd.tensor_tensor(q_lo[:, :], q[:, :], q_hi[:, :].bitcast(F32), ALU.subtract).then_inc(q_lo_ready, 1)
                if a == 10:
                    pool.wait_ge(vb_in, 16 * (m + 1))
                    if m >= 1:
                        pool.wait_ge(av_done, 8 * m)
                    for st in range(HALF):
                        dst = vz[:, st, :].rearrange("p (h c) -> p h c", h=HEADS)[:, :, 0:CH]
                        ins = nc.gpsimd.tensor_copy(dst, vb[:, st, :].rearrange("p (h c) -> p h c", h=HEADS))
                    ins.then_inc(vz_ready, 1)
                if a == 30:
                    norm_scale(var4_ready, m + 1, rstd4[:, :], ve4[:, :], 1, rstd4_ready)
                if a == 35:
                    pool.wait_ge(square_ready, m + 1)
                    nc.gpsimd.tensor_tensor(sc[:, 1:2], sc[:, 0:1], pos_half[:, :], ALU.pow).then_inc(norm_ready, 1)

            def wkv(n, w):
                if w == 0:
                    norm_scale(var_ready, 2 * n + 1, rstd[:, :], ve[:, :], BB, rstd_ready)
                if w == 30:
                    norm_scale(var_ready, 2 * n + 2, rstd[:, :], ve[:, :], BB, rstd_ready)
                for h in range(HALF):
                    c = 2 * n + h
                    if w == 7 + WKV_HALF * h:
                        pool.wait_ge(top_ready, c + 1)
                        nc.gpsimd.tensor_tensor(keep[:, :, :], top[:, :, 0:POS], top[:, :, 1:POS + 1],
                                                ALU.subtract).then_inc(gaps_ready, 1)
                        nc.gpsimd.tensor_tensor(take[:, :, :], kT[h][:, :, :], top[:, :, 1:POS + 1],
                                                ALU.subtract).then_inc(gaps_ready, 1)
                    if w == 9 + WKV_HALF * h:
                        if c == 0:
                            pool.wait_ge(v_in, 32)
                        elif h == 0:
                            pool.wait_ge(v_in, 32 * (n + 1))
                        pool.wait_ge(exps_ready, 3 * c + 3)
                        nc.gpsimd.tensor_tensor(take_v[:, :, :], take[:, :, :], vT[:, h, :, :], ALU.mult).then_inc(vs_ready, 1)
                        nc.gpsimd.tensor_tensor(now_v[:, :, :], now[:, :, :], vT[:, h, :, :], ALU.mult).then_inc(vs_ready, 1)

            for slot in range(FIRST_SLOT, LAST_SLOT + 1):
                moe(slot)
                weights(slot)
                for m, a in attn_steps(slot):
                    attention(m, a)
                for n, w in wkv_steps(slot):
                    wkv(n, w)

        @block.scalar
        def _(act):
            def moe(slot):
                t, r = slot // 3, slot % 3
                if 0 <= t < TILES * BLOCKS:
                    if r == 0:
                        act.wait_ge(gate_ready, t + 1)
                        if t >= 1:
                            act.wait_ge(gate_used, t)
                        nc.scalar.activation(th[:, :], gate_ps[:, :], ACT.Tanh, scale=0.5 / W_SCALE).then_inc(tanh_ready, 1)
                    if r == 2:
                        act.wait_ge(h_ready, t + 1)
                        if t >= 2:
                            act.wait_ge(y_done, t - 1)
                        nc.scalar.activation(h_hi[t % 2][:, :], hb[t % 2][:, :], ACT.Copy).then_inc(h_hi_ready, 1)
                n = slot // SLOTS - 1
                if 0 <= n < BLOCKS and slot % SLOTS == 2:
                    act.wait_ge(y_done, TILES * (n + 1))
                    if n >= 1:
                        act.wait_ge(y_turned, n)
                    for c in range(HALF):
                        nc.scalar.activation(ysb[:, c, :], y_ps[c][:, :], ACT.Copy,
                                             scale=1.0 / (H_SCALE * W_SCALE)).then_inc(y_copied, 1)

            def weights(slot):
                if slot % 3 == 0 and 0 <= slot // 3 + 3 < TILES:
                    j = slot // 3 + 3
                    act.wait_ge(stage_in[j % 3], 16 * (j // 3 + 1))
                    nc.scalar.activation(w13_hi[:, j, :, :, :].rearrange("p a b c -> p (a b c)"),
                                         stage[j % 3][:, 0:2 * FEAT], ACT.Copy, scale=W_SCALE).then_inc(w13_hi_ready, 1)
                    act.wait_ge(w13_lo_ready, j + 1)
                    nc.scalar.activation(w2_hi[:, j, :], stage[j % 3][:, 2 * FEAT:3 * FEAT], ACT.Copy).then_inc(w2_hi_ready, 1)

            def attention(m, a):
                i = m % 2
                if a == 1:
                    act.wait_ge(q_ready, m + 1)
                    if m >= 1:
                        act.wait_ge(q_out[(m - 1) % 2], 32 * ((m - 1) // 2 + 1))
                    nc.scalar.activation(q_hi[:, :], q[:, :], ACT.Copy).then_inc(q_hi_ready, 1)
                if a == 2:
                    act.wait_ge(kraw_in, 16 * (m + 1))
                    if m >= 2:
                        act.wait_ge(score_written, score_no[("exp", m - 2, 7)])
                    nc.scalar.activation(ks[i][0:STACK, :, :], kraw, ACT.Copy).then_inc(ks_hi_ready, 1)
                if a == 14:
                    act.wait_ge(misc_written, misc_no[("shift", m)])
                    if m >= 1:
                        act.wait_ge(shift_out, 16 * m)
                    nc.scalar.activation(shift[:, :], misc_ps[0:HEADS, 0:FEAT], ACT.Copy, scale=-1.0).then_inc(misc_read, 1)
                if 18 <= a < 26:
                    e = a - 18
                    no = score_no[("exp", m, e)]
                    act.wait_ge(score_written, no)
                    if 8 * m + e >= 2:
                        act.wait_ge(av_done, 8 * m + e - 1)
                    nc.scalar.activation(pr[e % 2][:, :], score_ps[:, :], ACT.Exp, scale=1.0 / CH).then_inc(score_read, 1)
                if a == 27:
                    act.wait_ge(av_done, 8 * (m + 1))
                    if m == 0:
                        act.wait_ge(consts_set, N_SET)
                    nc.scalar.activation(sums[96:96 + PAIRS, :], av_ps[96:96 + PAIRS, 0:FEAT], ACT.Copy).then_inc(sums_set, 1)
                    nc.scalar.activation(sums[0:PAIRS, :], av_ps[0:PAIRS, FEAT:2 * FEAT], ACT.Copy).then_inc(sums_set, 1)
                if a == 32:
                    act.wait_ge(misc_written, misc_no[("x4", m)])
                    nc.scalar.activation(x4T[:, :, :], misc_ps[:, 0:FEAT].rearrange("p (h t) -> p h t", h=HALF),
                                         ACT.Copy).then_inc(misc_read, 1)
                if a == 36:
                    act.wait_ge(norm1_ready, m + 1)
                    nc.scalar.activation(sc[:, 3:4], sc[:, 2:3], ACT.Tanh).then_inc(tanh1_ready, 1)

            def wkv(n, w):
                for h in range(HALF):
                    c = 2 * n + h
                    if w == 3 + h:
                        act.wait_ge(misc_written, misc_no[("k", n, h)])
                        nc.scalar.activation(kT[h][:, :, :], misc_ps[:, :].rearrange("p (b t) -> p b t", b=BB),
                                             ACT.Copy).then_inc(misc_read, 1)
                    if w == 8 + WKV_HALF * h:
                        if c == 0:
                            act.wait_ge(early_in, 16 * N_EARLY)
                        act.wait_ge(gaps_ready, 2 * c + 2)
                        nc.scalar.activation(keep[:, :, :], keep[:, :, :], ACT.Exp, bias=wu[:, h, 0:1]).then_inc(exps_ready, 1)
                        nc.scalar.activation(take[:, :, :], take[:, :, :], ACT.Exp).then_inc(exps_ready, 1)
                        act.wait_ge(own_ready, c + 1)
                        nc.scalar.activation(now[:, :, :], now[:, :, :], ACT.Exp).then_inc(exps_ready, 1)
                    if w == 33 + 2 * h:
                        if n >= 2:
                            act.wait_ge(up_ready, TILES * (n - 1))
                        act.wait_ge(misc_written, misc_no[("x2", n, h)])
                        nc.scalar.activation(xT_hi[n % 2][:, h, :], misc_ps[:, :], ACT.Copy).then_inc(x2_hi_ready, 1)
                if w == 38:
                    act.wait_ge(misc_read, misc_no[("gate", n)])
                    nc.scalar.activation(ex[:, :, :], lg[:, :, :], ACT.Exp, scale=1.0 / W_SCALE).then_inc(logits_exp, 1)
                if w == 46:
                    act.wait_ge(misc_written, misc_no[("route", n)])
                    nc.scalar.activation(cT[n % 2][:, :], misc_b[0:96, 0:TOK], ACT.Copy).then_inc(misc_read, 1)

            act.wait_ge(early_in, 16 * N_EARLY)
            nc.scalar.activation(gw_hi[:, :, :], gw[:, :, :], ACT.Copy, scale=W_SCALE).then_inc(gate_w_hi, 1)
            for slot in range(FIRST_SLOT, LAST_SLOT + 1):
                moe(slot)
                weights(slot)
                for m, a in attn_steps(slot):
                    attention(m, a)
                for n, w in wkv_steps(slot):
                    wkv(n, w)

        @block.vector
        def _(dve):
            steps = [0]

            def link(ins):
                steps[0] += 1
                ins.then_inc(dve_step, 1)
                dve.wait_ge(dve_step, steps[0])

            def norm_stats(xs, st, mean_var, var_eps, var_ready):
                for b, xb in enumerate(xs):
                    ins = nc.vector.bn_stats(st[b], xb)
                link(ins)
                for b in range(len(xs)):
                    ins = nc.vector.bn_aggr(mean_var[b], st[b])
                link(ins)
                nc.vector.tensor_scalar(var_eps[0], var_eps[1], LN_EPS, None, ALU.add).then_inc(var_ready, 1)

            def moe(slot):
                t, r = slot // 3, slot % 3
                if 0 <= t < TILES * BLOCKS:
                    if r == 0:
                        dve.wait_ge(tanh_ready, t + 1)
                        nc.vector.scalar_tensor_tensor(t1[:, :], th[:, :], 1.0, gate_ps[:, :], ALU.add,
                                                       ALU.mult).then_inc(gate_used, 1)
                    if r == 1:
                        dve.wait_ge(gate_used, t + 1)
                        dve.wait_ge(route_ready, t + 1)
                        nc.vector.tensor_tensor(t1[:, :], t1[:, :], route_ps[:, :], ALU.mult).then_inc(route_used, 1)
                        dve.wait_ge(route_used, t + 1)
                        dve.wait_ge(up_ready, t + 1)
                        if t >= 2:
                            dve.wait_ge(h_lo_ready, t - 1)
                        nc.vector.tensor_tensor(hb[t % 2][:, :], t1[:, :], up_ps[:, :], ALU.mult).then_inc(h_ready, 1)
                n = slot // SLOTS - 1
                if 0 <= n < BLOCKS and slot % SLOTS == 4:
                    dve.wait_ge(y_turned, n + 1)
                    for c in range(2):
                        part = res[n % 3][:, 2 * c:2 * c + 2, :]
                        ins = nc.vector.tensor_tensor(part, part, y_ps[c][:, :].rearrange("p (b f) -> p b f", b=2), ALU.add)
                    ins.then_inc(y_added, 1)
                    dve.wait_ge(y_added, n + 1)

            def weights(slot):
                if slot % 3 == 0 and 0 <= slot // 3 + 3 < TILES:
                    j = slot // 3 + 3
                    dve.wait_ge(stage_in[j % 3], 16 * (j // 3 + 1))
                    part = stage[j % 3][:, 2 * FEAT:3 * FEAT]
                    nc.vector.tensor_scalar(part, part, W_SCALE, None, ALU.mult)
                    dve.wait_ge(w13_hi_ready, j + 1)
                    nc.vector.scalar_tensor_tensor(w13_lo[:, j, :, :, :].rearrange("p a b c -> p (a b c)"),
                                                   stage[j % 3][:, 0:2 * FEAT], W_SCALE,
                                                   w13_hi[:, j, :, :, :].rearrange("p a b c -> p (a b c)"),
                                                   ALU.mult, ALU.subtract).then_inc(w13_lo_ready, 1)

            def attention(m, a):
                xb = res[(m // BB) % 3][:, m % BB, :]
                if a == 0:
                    norm_stats([xb], [stats3[:, :]], [mv3[:, :]], (ve3[:, :], mv3[:, 1:2]), var3_ready)
                if a == 1:
                    dve.wait_ge(rstd3_ready, m + 1)
                    if m >= 1:
                        dve.wait_ge(q_lo_ready, m)
                    nc.vector.tensor_scalar(q[:, :], xb, mv3[:, 0:1], rstd3[:, 0:1], ALU.subtract, ALU.mult).then_inc(q_ready, 1)
                if a == 3:
                    dve.wait_ge(ks_hi_ready, m + 1)
                    low = ks[m % 2][64:STACK, :, :]
                    nc.vector.tensor_tensor(low, kraw[64:STACK, :, :], low.bitcast(F32), ALU.subtract).then_inc(ks_ready, 1)
                if 6 <= a < 14:
                    v = a - 6
                    p, tt = v // 2, v % 2
                    no = score_no[("max", m, v)]
                    dve.wait_ge(score_written, no)
                    dst = mx[:, tt, :].rearrange("q (a p) -> q a p", a=2)[:, :, p]
                    nc.vector.tensor_reduce(dst, score_ps[:, :].rearrange("q (a k) -> q a k", a=2), AX_X,
                                            ALU.max).then_inc(score_read, 1)
                if a == 28:
                    dve.wait_ge(misc_written, misc_no[("sums", m)])
                    nc.vector.reciprocal(rsum[:, :], misc_ps[:, 0:FEAT]).then_inc(misc_read, 1)
                    dve.wait_ge(misc_read, misc_no[("sums", m)])
                if a == 29:
                    x_lo, x_hi = res[(m // BB) % 3][0:64, m % BB, :], res[(m // BB) % 3][64:P, m % BB, :]
                    nc.vector.tensor_tensor(rsum[0:64, :], rsum[0:64, :], av_ps[0:64, 0:FEAT], ALU.mult)
                    nc.vector.tensor_tensor(rsum[64:P, :], rsum[64:P, :], av_ps[64:P, FEAT:2 * FEAT], ALU.mult).then_inc(av_read, 1)
                    dve.wait_ge(av_read, m + 1)
                    link(nc.vector.tensor_tensor(xb, xb, rsum[:, :], ALU.add))
                if a == 30:
                    norm_stats([xb], [stats4[:, :]], [mv4[:, :]], (ve4[:, :], mv4[:, 1:2]), var4_ready)
                if a == 31:
                    dve.wait_ge(rstd4_ready, m + 1)
                    nc.vector.tensor_scalar(x4n[:, :], xb, mv4[:, 0:1], rstd4[:, 0:1], ALU.subtract, ALU.mult).then_inc(x4_ready, 1)
                if a == 33:
                    dve.wait_ge(misc_written, misc_no[("ffn", m)])
                    if m == 0:
                        dve.wait_ge(consts_in, 16 * N_CONSTS)
                    nc.vector.tensor_tensor(fo[:, :], misc_ps[:, 0:FEAT], ffn_s[:, :], ALU.mult).then_inc(misc_read, 1)
                    dve.wait_ge(misc_read, misc_no[("ffn", m)])
                    nc.vector.tensor_tensor_reduce(x4n[:, :], fo[:, :], fo[:, :], 1.0, 0.0, ALU.mult, ALU.add,
                                                   sc[:, 0:1]).then_inc(square_ready, 1)
                if a == 35:
                    dve.wait_ge(norm_ready, m + 1)
                    nc.vector.tensor_scalar(sc[:, 2:3], sc[:, 1:2], BALL_EPS, None, ALU.max).then_inc(norm1_ready, 1)
                    dve.wait_ge(norm1_ready, m + 1)
                    link(nc.vector.tensor_scalar(sc[:, 4:5], sc[:, 2:3], BALL_EPS, None, ALU.add))
                    link(nc.vector.reciprocal(sc[:, 5:6], sc[:, 4:5]))
                if a == 37:
                    dve.wait_ge(tanh1_ready, m + 1)
                    link(nc.vector.tensor_tensor(sc[:, 6:7], sc[:, 3:4], sc[:, 5:6], ALU.mult))
                    link(nc.vector.tensor_tensor(sc[:, 7:8], sc[:, 1:2], sc[:, 6:7], ALU.mult))
                    link(nc.vector.tensor_scalar(sc[:, 8:9], sc[:, 7:8], BALL_EPS, None, ALU.max))
                    link(nc.vector.reciprocal(sc[:, 9:10], sc[:, 8:9]))
                    link(nc.vector.tensor_scalar(sc[:, 10:11], sc[:, 9:10], MAX_NORM, 1.0, ALU.mult, ALU.min))
                    link(nc.vector.tensor_tensor(sc[:, 11:12], sc[:, 10:11], sc[:, 6:7], ALU.mult))
                    nc.vector.scalar_tensor_tensor(xb, fo[:, :], sc[:, 11:12], xb, ALU.mult, ALU.add).then_inc(res_ready, 1)

            def block_norm(n, k):
                r = res[n % 3]
                norm_stats([r[:, b, :] for b in range(BB)], [stats[:, b, :] for b in range(BB)],
                           [mv[:, b, :] for b in range(BB)], (ve[:, :], mv[:, :, 1]), var_ready)

            def block_normed(n, k):
                dve.wait_ge(rstd_ready, 2 * n + k + 1)
                for b in range(BB):
                    ins = nc.vector.tensor_scalar(xn[:, b, :], res[n % 3][:, b, :], mv[:, b, 0:1], rstd[:, b:b + 1],
                                                  ALU.subtract, ALU.mult)
                ins.then_inc(xn_ready, 1)

            def wkv(n, w):
                if w == 0:
                    dve.wait_ge(x_in, 16 * (n + 1))
                    block_norm(n, 0)
                if w == 1:
                    if n >= 1:
                        dve.wait_ge(misc_written, misc_no[("x2", n - 1, 1)])
                    block_normed(n, 0)
                for h in range(HALF):
                    c = 2 * n + h
                    u = w - WKV_HALF * h
                    if u == 6:
                        if c == 0:
                            dve.wait_ge(early_in, 16 * N_EARLY)
                            dve.wait_ge(consts_set, N_SET)
                        dve.wait_ge(misc_read, misc_no[("k", n, h)])
                        for b in range(BB):
                            ins = nc.vector.tensor_tensor_scan(top[:, b, 1:POS + 1], wu[:, h, 0:1].to_broadcast([P, POS]),
                                                               kT[h][:, b, :], NEG, ALU.add, ALU.max)
                        ins.then_inc(top_ready, 1)
                        dve.wait_ge(top_ready, c + 1)
                    if u == 7:
                        link(nc.vector.scalar_tensor_tensor(now[:, :, :], kT[h][:, :, :], wu[:, h, 1:2], top[:, :, 0:POS],
                                                            ALU.add, ALU.subtract))
                        nc.vector.tensor_scalar(now[:, :, :], now[:, :, :], CLAMP, None, ALU.min).then_inc(own_ready, 1)
                    if u == 8:
                        dve.wait_ge(exps_ready, 3 * c + 3)
                        for b in range(BB):
                            nc.vector.tensor_tensor_scan(den_s[:, b, 1:POS + 1], keep[:, b, :], take[:, b, :], 0.0,
                                                         ALU.mult, ALU.add)
                    if u == 10:
                        dve.wait_ge(vs_ready, 2 * c + 2)
                        for b in range(BB):
                            ins = nc.vector.tensor_tensor_scan(num_s[:, b, 1:POS + 1], keep[:, b, :], take_v[:, b, :], 0.0,
                                                               ALU.mult, ALU.add)
                        link(ins)
                    if u == 11:
                        if c >= 1:
                            dve.wait_ge(misc_written, misc_no[("y", (c - 1) // 2, (c - 1) % 2)])
                        nc.vector.tensor_tensor(yk[:, :, :], num_s[:, :, 0:POS], now_v[:, :, :], ALU.add)
                        link(nc.vector.tensor_tensor(now[:, :, :], den_s[:, :, 0:POS], now[:, :, :], ALU.add))
                    if u in (12, 13):
                        lo = 2 * (u - 12)
                        link(nc.vector.reciprocal(now[:, lo:lo + 2, :], now[:, lo:lo + 2, :]))
                    if u == 14:
                        nc.vector.tensor_tensor(yk[:, :, :], yk[:, :, :], now[:, :, :], ALU.mult).then_inc(yk_ready, 1)
                    if u == 16:
                        dve.wait_ge(misc_written, misc_no[("y", n, h)])
                        part = res[n % 3][:, :, h * P:(h + 1) * P]
                        nc.vector.tensor_tensor(part, part, misc_ps[:, :].rearrange("p (b f) -> p b f", b=BB),
                                                ALU.add).then_inc(misc_read, 1)
                if w == 30:
                    dve.wait_ge(misc_read, misc_no[("y", n, 1)])
                    block_norm(n, 1)
                if w == 31:
                    block_normed(n, 1)
                for h in range(HALF):
                    if w == 33 + 2 * h:
                        dve.wait_ge(x2_hi_ready, 2 * n + h + 1)
                        nc.vector.tensor_tensor(xT_lo[n % 2][:, h, :], misc_ps[:, :], xT_hi[n % 2][:, h, :],
                                                ALU.subtract).then_inc(misc_read, 1)
                if w == 38:
                    dve.wait_ge(misc_written, misc_no[("gate", n)])
                    logits = misc_ps[:, 0:BB * EXPERTS].rearrange("p (b e) -> p b e", b=BB)
                    link(nc.vector.tensor_reduce(lmax[:, :], logits, AX_X, ALU.max))
                    nc.vector.tensor_tensor(lg[:, :, :], logits, lmax[:, :].unsqueeze(2).to_broadcast([P, BB, EXPERTS]),
                                            ALU.subtract).then_inc(misc_read, 1)
                if w == 40:
                    dve.wait_ge(logits_exp, n + 1)
                    link(nc.vector.tensor_reduce(small[:, 0, :], ex[:, :, :], AX_X, ALU.add))
                    link(nc.vector.reciprocal(small[:, 1, :], small[:, 0, :]))
                    link(nc.vector.tensor_tensor(probs[:, :, 0:EXPERTS], ex[:, :, :],
                                                 small[:, 1, :].unsqueeze(2).to_broadcast([P, BB, EXPERTS]), ALU.mult))
                if w == 41:
                    for b in range(BB):
                        ins = nc.vector.max(top8[:, b, :], probs[:, b, :])
                    link(ins)
                    for b in range(BB):
                        ins = nc.vector.match_replace(rest[:, b, :], top8[:, b, :], probs[:, b, :], 0.0)
                    link(ins)
                if w == 42:
                    link(nc.vector.tensor_tensor(route[:, :, :], probs[:, :, 0:EXPERTS], rest[:, :, 0:EXPERTS], ALU.subtract))
                    link(nc.vector.tensor_reduce(small[:, 2, :], route[:, :, :], AX_X, ALU.add))
                    link(nc.vector.tensor_scalar(small[:, 2, :], small[:, 2, :], 1e-20, None, ALU.add))
                    link(nc.vector.reciprocal(small[:, 3, :], small[:, 2, :]))
                    link(nc.vector.tensor_scalar(small[:, 3, :], small[:, 3, :], ROUTE_SCALE, None, ALU.mult))
                    link(nc.vector.tensor_tensor(route[:, :, :], route[:, :, :],
                                                 small[:, 3, :].unsqueeze(2).to_broadcast([P, BB, EXPERTS]), ALU.mult))
                if w == 43:
                    if n >= 1:
                        dve.wait_ge(misc_written, misc_no[("route", n - 1)])
                    link(nc.vector.tensor_copy(route3[:, :, 0:EXPERTS], route[:, :, :]))
                    link(nc.vector.tensor_tensor(route[:, :, :], route[:, :, :], route3[:, :, 0:EXPERTS], ALU.subtract))
                    link(nc.vector.tensor_copy(route3[:, :, 32:32 + EXPERTS], route[:, :, :]))
                    link(nc.vector.tensor_tensor(route[:, :, :], route[:, :, :], route3[:, :, 32:32 + EXPERTS], ALU.subtract))
                    nc.vector.tensor_copy(route3[:, :, 64:64 + EXPERTS], route[:, :, :]).then_inc(split_ready, 1)

            for i in range(2):
                nc.vector.memset(ks[i][STACK:P, :, :].bitcast(F32), 1.0).then_inc(consts_set, 1)
            dve.wait_ge(gate_w_hi, 1)
            nc.vector.scalar_tensor_tensor(gw_lo[:, :, :], gw[:, :, :], W_SCALE, gw_hi[:, :, :], ALU.mult,
                                           ALU.subtract).then_inc(gate_w_lo, 1)
            for slot in range(FIRST_SLOT, LAST_SLOT + 1):
                moe(slot)
                weights(slot)
                for m, a in attn_steps(slot):
                    attention(m, a)
                for n, w in wkv_steps(slot):
                    wkv(n, w)

        @block.tensor
        def _(pe):
            def misc_free(key):
                if misc_no[key] > 1:
                    pe.wait_ge(misc_read, misc_no[key] - 1)

            def score_free(key):
                if score_no[key] > 1:
                    pe.wait_ge(score_read, score_no[key] - 1)

            def rows(bank_ap, n, j, gu):
                i = n % 2
                for k in range(HALF):
                    for wt, xt in ((w13_hi, xT_hi), (w13_lo, xT_hi), (w13_hi, xT_lo)):
                        last = k == HALF - 1 and xt is xT_lo
                        ins = nc.tensor.matmul(bank_ap, wt[:, j, gu, k, :], xt[i][:, k, :],
                                               start=(k == 0 and wt is w13_hi and xt is xT_hi), stop=last)
                return ins

            def down(t):
                n, j = t // TILES, t % TILES
                pe.wait_ge(h_lo_ready, t + 1)
                if n == 0:
                    pe.wait_ge(w2_lo_ready, j + 1)
                elif j == 0:
                    pe.wait_ge(y_added, n)
                for c in range(HALF):
                    cols = slice(c * P, (c + 1) * P)
                    nc.tensor.matmul(y_ps[c][:, :], w2_hi[:, j, cols], h_hi[t % 2][:, :], start=(j == 0), stop=False)
                    nc.tensor.matmul(y_ps[c][:, :], w2_lo[:, j, cols], h_hi[t % 2][:, :], start=False, stop=False)
                    ins = nc.tensor.matmul(y_ps[c][:, :], w2_hi[:, j, cols], h_lo[t % 2][:, :], start=False,
                                           stop=(j == TILES - 1))
                ins.then_inc(y_done, 1)

            def moe(slot):
                t, r = slot // 3, slot % 3
                n, j = t // TILES, t % TILES
                if 0 <= t < TILES * BLOCKS:
                    if r == 0:
                        if j == 0:
                            pe.wait_ge(misc_read, misc_no[("x2", n, 1)])
                        if n == 0:
                            pe.wait_ge(w13_lo_ready, j + 1)
                        if t >= 1:
                            pe.wait_ge(gate_used, t)
                        rows(gate_ps[:, :], n, j, 0).then_inc(gate_ready, 1)
                    if r == 1:
                        if j == 0:
                            pe.wait_ge(misc_read, misc_no[("route", n)])
                        if t >= 1:
                            pe.wait_ge(route_used, t)
                        nc.tensor.matmul(route_ps[:, :], rows_sb[:, j * P:(j + 1) * P], cT[n % 2][:, :], start=True,
                                         stop=True).then_inc(route_ready, 1)
                        if t >= 1:
                            pe.wait_ge(h_ready, t)
                        rows(up_ps[:, :], n, j, 1).then_inc(up_ready, 1)
                if r == 2 and 0 <= t - 1 < TILES * BLOCKS:
                    down(t - 1)
                b = slot // SLOTS - 1
                if 0 <= b < BLOCKS and slot % SLOTS == 4:
                    pe.wait_ge(y_copied, 2 * (b + 1))
                    for bb in range(BB):
                        for c in range(HALF):
                            col = (bb % 2) * FEAT + c * P
                            ins = nc.tensor.transpose(y_ps[bb // 2][:, col:col + P], ysb[:, c, bb * P:(bb + 1) * P], eye_sb[:, :])
                    ins.then_inc(y_turned, 1)

            def attention(m, a):
                i = m % 2
                if 6 <= a < 14:
                    v = a - 6
                    p, tt = v // 2, v % 2
                    if v == 0:
                        pe.wait_ge(qz_in[i], 96 * (m // 2 + 1))
                        pe.wait_ge(ks_ready, m + 1)
                    score_free(("max", m, v))
                    for half in range(2):
                        col = half * FEAT + tt * P
                        ins = nc.tensor.matmul(score_ps[:, half * FEAT:(half + 1) * FEAT], qz[i][0:STACK, p, col:col + P],
                                               ks[i][0:STACK, p, :], start=True, stop=True)
                    ins.then_inc(score_written, 1)
                if a == 14:
                    misc_free(("shift", m))
                    pe.wait_ge(score_read, score_no[("max", m, 7)])
                    for tt in range(HALF):
                        ins = nc.tensor.transpose(misc_ps[0:HEADS, tt * P:(tt + 1) * P], mx[:, tt, :], eye_sb[:, :])
                    ins.then_inc(misc_written, 1)
                if 18 <= a < 26:
                    e = a - 18
                    p, st = e // 2, e % 2
                    if e == 0:
                        pe.wait_ge(shift_in, 32 * (m + 1))
                    score_free(("exp", m, e))
                    nc.tensor.matmul(score_ps[:, :], ks[i][0:STACK + 2, p, st * P:(st + 1) * P], qz[i][0:STACK + 2, p, :],
                                     start=True, stop=True).then_inc(score_written, 1)
                if 19 <= a < 27:
                    e = a - 19
                    p, st = e // 2, e % 2
                    if e == 0:
                        pe.wait_ge(vz_ready, m + 1)
                        if m >= 1:
                            pe.wait_ge(av_read, m)
                    pe.wait_ge(score_read, score_no[("exp", m, e)])
                    nc.tensor.matmul(av_ps[:, 0:FEAT], heads_view(vz, st, p), pr[e % 2][:, 0:FEAT], start=(e == 0),
                                     stop=(e == 7), skip_group_check=True)
                    nc.tensor.matmul(av_ps[:, FEAT:2 * FEAT], heads_view(vz, st, p + PAIRS), pr[e % 2][:, FEAT:2 * FEAT],
                                     start=False, stop=(e == 7), skip_group_check=True).then_inc(av_done, 1)
                if a == 28:
                    misc_free(("sums", m))
                    pe.wait_ge(sums_set, 2 * (m + 1))
                    nc.tensor.matmul(misc_ps[:, 0:FEAT], sums_sb[:, :], sums[:, :], start=True, stop=True).then_inc(misc_written, 1)
                if a == 32:
                    misc_free(("x4", m))
                    pe.wait_ge(x4_ready, m + 1)
                    for h in range(HALF):
                        ins = nc.tensor.transpose(misc_ps[:, h * P:(h + 1) * P], x4n[:, h * P:(h + 1) * P], eye_sb[:, :])
                    ins.then_inc(misc_written, 1)
                if a == 33:
                    misc_free(("ffn", m))
                    pe.wait_ge(misc_read, misc_no[("x4", m)])
                    for h in range(HALF):
                        ins = nc.tensor.matmul(misc_ps[:, 0:FEAT], x4T[:, h, :], ffn_sb[:, h, :], start=(h == 0), stop=(h == HALF - 1))
                    ins.then_inc(misc_written, 1)

            def wkv(n, w):
                for h in range(HALF):
                    if w == 3 + h:
                        misc_free(("k", n, h))
                        pe.wait_ge(xn_ready, 2 * n + 1)
                        for b in range(BB):
                            ins = nc.tensor.transpose(misc_ps[:, b * P:(b + 1) * P], xn[:, b, h * P:(h + 1) * P], eye_sb[:, :])
                        ins.then_inc(misc_written, 1)
                    if w == 16 + WKV_HALF * h:
                        misc_free(("y", n, h))
                        pe.wait_ge(yk_ready, 2 * n + h + 1)
                        for b in range(BB):
                            ins = nc.tensor.transpose(misc_ps[:, b * P:(b + 1) * P], yk[:, b, :], eye_sb[:, :])
                        ins.then_inc(misc_written, 1)
                    if w == 33 + 2 * h:
                        misc_free(("x2", n, h))
                        pe.wait_ge(xn_ready, 2 * n + 2)
                        for b in range(BB):
                            ins = nc.tensor.transpose(misc_ps[:, b * P:(b + 1) * P], xn[:, b, h * P:(h + 1) * P], eye_sb[:, :])
                        ins.then_inc(misc_written, 1)
                if w == 38:
                    misc_free(("gate", n))
                    pe.wait_ge(gate_w_lo, 1)
                    i = n % 2
                    for b in range(BB):
                        for k in range(HALF):
                            tok = slice(b * P, (b + 1) * P)
                            for xt, wt in ((xT_hi, gw_hi), (xT_lo, gw_hi), (xT_hi, gw_lo)):
                                ins = nc.tensor.matmul(misc_ps[:, b * EXPERTS:(b + 1) * EXPERTS], xt[i][:, k, tok], wt[:, k, :],
                                                       start=(k == 0 and xt is xT_hi and wt is gw_hi),
                                                       stop=(k == HALF - 1 and wt is gw_lo))
                    ins.then_inc(misc_written, 1)
                if w == 46:
                    misc_free(("route", n))
                    pe.wait_ge(split_ready, n + 1)
                    for b in range(BB):
                        ins = nc.tensor.transpose(misc_b[0:96, b * P:(b + 1) * P], route3[:, b, :], eye_b_sb[:, :])
                    ins.then_inc(misc_written, 1)

            pe.wait_ge(early_in, 16 * N_EARLY)
            pe.wait_ge(consts_in, 16 * N_CONSTS)
            pe.wait_ge(consts_set, N_SET)
            for slot in range(FIRST_SLOT, LAST_SLOT + 1):
                moe(slot)
                for m, a in attn_steps(slot):
                    attention(m, a)
                for n, w in wkv_steps(slot):
                    wkv(n, w)


def expert_rows():
    import numpy as np
    sel = np.zeros((96, TILES * P), np.uint16)
    for r in range(EXPERTS * INNER + SHARED):
        e = min(r // INNER, EXPERTS)
        sel[e, r] = BF16_ONE
        if e < EXPERTS:
            sel[32 + e, r] = sel[64 + e, r] = BF16_ONE
    return sel


def head_sums():
    import numpy as np
    sel = np.zeros((P, P), np.float32)
    for w in range(POS):
        h = w // CH
        sel[96 + h if h < PAIRS else h - PAIRS, w] = 1
    return sel


def kernel(x, ctx_2048, L0_xattn_w, L0_xattn_u, L0_ffn_gate_w, L0_ffn_w13, L0_ffn_w2, L0_ffn_sw13, L0_ffn_sw2,
           L1_ffn_weight, L1_ffn_scale):
    import numpy as np
    import concourse.bacc as bacc
    from concourse.bass_utils import run_bass_kernel_spmd

    def arr(a):
        return np.asarray(a)

    x, c = arr(x), arr(ctx_2048)
    heads = c.reshape(BATCH, 2, PAIRS, CH, FEAT).transpose(0, 1, 3, 2, 4)
    a, b = heads[:, 0], heads[:, 1]
    ctx_heads = np.concatenate([a, a, b, b, a, b], axis=1)

    def inner(w):
        rows = np.concatenate([w, np.zeros((TILES * P - w.shape[0], FEAT), w.dtype)])
        return rows.reshape(TILES, P, HALF, P).transpose(0, 3, 2, 1)

    w13, sw13 = arr(L0_ffn_w13), arr(L0_ffn_sw13)
    gate = inner(np.concatenate([w13[:, :INNER].reshape(-1, FEAT), sw13[:SHARED]]))
    up = inner(np.concatenate([w13[:, INNER:].reshape(-1, FEAT), sw13[SHARED:]]))
    w2 = np.concatenate([arr(L0_ffn_w2).transpose(0, 2, 1).reshape(-1, FEAT), arr(L0_ffn_sw2).T])
    w2 = np.concatenate([w2, np.zeros((TILES * P - w2.shape[0], FEAT), w2.dtype)]).reshape(TILES, P, FEAT)
    experts = np.concatenate([gate.reshape(TILES, P, FEAT), up.reshape(TILES, P, FEAT), w2], axis=2)

    arrays = {
        "x": x,
        "ctx_feat": c.transpose(0, 2, 1),
        "ctx_heads": ctx_heads,
        "experts": experts,
        "gate_w": arr(L0_ffn_gate_w).T.reshape(HALF, P, EXPERTS).transpose(1, 0, 2),
        "decay_bonus": np.stack([arr(L0_xattn_w), arr(L0_xattn_u)], 1).reshape(HALF, P, 2).transpose(1, 0, 2),
        "ffn_w": arr(L1_ffn_weight).reshape(HALF, P, FEAT).transpose(1, 0, 2),
        "ffn_scale": arr(L1_ffn_scale),
        "rows_of": expert_rows(),
        "sums_of": head_sums(),
        "eye": np.eye(P, dtype=np.float32),
        "eye_b": np.eye(P, dtype=np.uint16) * np.uint16(BF16_ONE),
    }
    arrays = {name: np.ascontiguousarray(v) for name, v in arrays.items()}
    nc = bacc.Bacc("TRN2", target_bir_lowering=False, num_devices=1)
    args = [nc.dram_tensor(name, v.shape, mybir.dt.from_np(v.dtype), kind="ExternalInput").ap() for name, v in arrays.items()]
    out = nc.dram_tensor("out", (BATCH, POS, FEAT), F32, kind="ExternalOutput").ap()
    build(nc, *args, out)
    r = run_bass_kernel_spmd(nc, [arrays], core_ids=[0])
    return r.results[0]["out"]
```

```python
from contextlib import ExitStack

import concourse.bass as bass
from concourse import mybir

F32 = mybir.dt.float32
F32R = mybir.dt.float32r
F16 = mybir.dt.float16
ALU = mybir.AluOpType
ACT = mybir.ActivationFunctionType
AX_X = mybir.AxisListType.X

P = 128
BATCH, POS, FEAT = 16, 128, 256
HALF = FEAT // P
BB = 4
BLOCKS = BATCH // BB
TOK = BB * POS
EXPERTS, INNER, TOP_K = 16, 176, 6
SHARED = 2 * INNER
TILES = -(-(EXPERTS * INNER + SHARED) // P)
HEADS = 8
CH = POS // HEADS
PAIRS = HEADS // 2
STACK = 6 * CH
LN_EPS = 1e-5
BALL_EPS = 1e-7
MAX_NORM = 0.99
NEG = -1e38
CLAMP = 60.0

W_SCALE = 64.0
H_SCALE = 8.0
ROUTE_SCALE = H_SCALE * 0.5 / (W_SCALE * W_SCALE)

SLOTS = 3 * TILES
WKV_START = 6 - SLOTS
K_TURN, HALVES, HALF_GAP, Y_TURN = 3, 6, 16, 18
X2_NORM, X2_TURN, GATE, TOP, ROUTE = 42, 46, 51, 53, 60
ATTN_GAP, ATTN_LAST_GAP = 18, 18
MAXIMA, SHIFT, EXPS, VALUES, VALUES_OUT, ATT_TURN, X4_TURN, FFN = 8, 17, 22, 25, 34, 35, 39, 41
V_SPLIT = 16
FIRST_SLOT = WKV_START
ATTN_LAST = FFN + 6
ROUTED = EXPERTS * INNER // P
LAST_SLOT = SLOTS * BLOCKS + 5 + ATTN_LAST_GAP * (BB - 1) + ATTN_LAST


def wkv_start(n):
    return WKV_START + SLOTS * n


def attn_start(m):
    gap = ATTN_LAST_GAP if m // BB == BLOCKS - 1 else ATTN_GAP
    return SLOTS * (m // BB + 1) + 5 + gap * (m % BB)


def attn_steps(slot):
    return [(m, slot - attn_start(m)) for m in range(BATCH) if 0 <= slot - attn_start(m) <= ATTN_LAST]


def wkv_steps(slot):
    return [(n, slot - wkv_start(n)) for n in range(BLOCKS) if 0 <= slot - wkv_start(n) < SLOTS]


def route_parts():
    parts, landed, had = [], [], [0, 0, 0]
    for r in range(ROUTED * BLOCKS):
        j = r % ROUTED
        cuts = []
        row = j * P
        while row < (j + 1) * P:
            e = row // INNER
            end = min((e + 1) * INNER, (j + 1) * P)
            cuts.append((e, row - j * P, end - j * P))
            row = end
        had[r % 3] += len(cuts)
        parts.append(cuts)
        landed.append(16 * had[r % 3])
    return parts, landed


def bank_uses():
    misc, score = {}, {}
    for slot in range(FIRST_SLOT, LAST_SLOT + 1):
        for m, a in attn_steps(slot):
            if MAXIMA <= a < MAXIMA + 8:
                score[("max", m, a - MAXIMA)] = len(score) + 1
            if a == SHIFT:
                misc[("shift", m)] = len(misc) + 1
            if EXPS <= a < EXPS + 8:
                score[("exp", m, a - EXPS)] = len(score) + 1
            if a == ATT_TURN:
                misc[("att", m)] = len(misc) + 1
            if a == X4_TURN:
                misc[("x4", m)] = len(misc) + 1
            if a == FFN:
                misc[("ffn", m)] = len(misc) + 1
        for n, w in wkv_steps(slot):
            for h in range(HALF):
                if w == K_TURN + h:
                    misc[("k", n, h)] = len(misc) + 1
                if w == HALVES + Y_TURN + HALF_GAP * h:
                    misc[("y", n, h)] = len(misc) + 1
                if w == X2_TURN + 2 * h:
                    misc[("x2", n, h)] = len(misc) + 1
            if w == GATE:
                misc[("gate", n)] = len(misc) + 1
            if w == ROUTE:
                misc[("route", n)] = len(misc) + 1
    return misc, score


def build(nc, x, ctx_feat, ctx_heads, experts, gate_w, decay_bonus, ffn_w, ffn_scale, eye, out):
    misc_no, score_no = bank_uses()
    score_of = {no: key for key, no in score_no.items()}
    parts, parts_in = route_parts()
    c_scratch = nc.dram_tensor("c_scratch", (2, EXPERTS, TOK), F32, kind="Internal").ap()
    q_scratch = nc.dram_tensor("q_scratch", (2, 2, P, FEAT), F32, kind="Internal").ap()
    m_scratch = nc.dram_tensor("m_scratch", (2, HEADS, FEAT), F32, kind="Internal").ap()

    with ExitStack() as ctx:
        def sb(name, shape, dt=F32):
            return ctx.enter_context(nc.sbuf_tensor(name, shape, dt))

        def bank(name):
            return ctx.enter_context(nc.psum_tensor(name, [P, 512], F32))

        w13_hi = sb("w13_hi", [P, TILES, 2, HALF, P], F16)
        w13_lo = sb("w13_lo", [P, TILES, 2, HALF, P], F16)
        w2_hi = sb("w2_hi", [P, TILES, FEAT], F16)
        w2_lo = sb("w2_lo", [P, TILES, FEAT], F16)
        gw = sb("gw", [P, HALF, EXPERTS])
        gw_hi = sb("gw_hi", [P, HALF, EXPERTS], F16)
        gw_lo = sb("gw_lo", [P, HALF, EXPERTS], F16)
        arena = sb("arena", [P, 9 * FEAT])
        stage = [arena[:, 3 * FEAT * i:3 * FEAT * (i + 1)] for i in range(3)]
        ysb = arena[:, 0:HALF * TOK].rearrange("p (h t) -> p h t", h=HALF)
        kraw = arena[0:STACK, 4 * FEAT:8 * FEAT].rearrange("p (a k) -> p a k", a=PAIRS)
        vb = arena[:, 8 * FEAT:9 * FEAT].rearrange("p (h t) -> p h t", h=HALF)
        eye_sb = sb("eye_sb", [P, P])
        wu = sb("wu", [P, HALF, 2])
        ffn_sb = sb("ffn_sb", [P, HALF, FEAT])
        ffn_s = sb("ffn_s", [P, FEAT])
        neg_half = sb("neg_half", [P, BB])
        pos_half = sb("pos_half", [P, 1])
        res = [sb(f"res{i}", [P, BB, FEAT]) for i in range(BLOCKS)]
        xn = sb("xn", [P, BB, FEAT])
        vT = sb("vT", [P, HALF, BB, POS])
        kT = [sb(f"kT{h}", [P, BB, POS]) for h in range(HALF)]
        top = sb("top", [P, BB, POS + 1])
        num_s = sb("num_s", [P, BB, POS + 1])
        den_s = sb("den_s", [P, BB, POS + 1])
        keep = sb("keep", [P, BB, POS])
        take = sb("take", [P, BB, POS])
        now = sb("now", [P, BB, POS])
        take_v = sb("take_v", [P, BB, POS])
        now_v = sb("now_v", [P, BB, POS])
        yk = take_v
        stats = sb("stats", [P, BB, 6])
        mv = sb("mv", [P, BB, 2])
        ve = sb("ve", [P, BB])
        rstd = sb("rstd", [P, BB])
        lg = sb("lg", [P, BB, EXPERTS])
        lmax = sb("lmax", [P, BB])
        ex = sb("ex", [P, BB, EXPERTS])
        small = sb("small", [P, 4, BB])
        probs = sb("probs", [P, BB, EXPERTS + 2])
        top8 = sb("top8", [P, BB, 8])
        rest = sb("rest", [P, BB, EXPERTS + 2])
        route = sb("route", [P, BB, EXPERTS])
        cT = sb("cT", [EXPERTS, TOK])
        cb = [sb(f"cb{i}", [P, TOK]) for i in range(3)]
        xT_hi = [sb(f"xT_hi{i}", [P, HALF, TOK], F16) for i in range(2)]
        xT_lo = [sb(f"xT_lo{i}", [P, HALF, TOK], F16) for i in range(2)]
        th = sb("th", [P, TOK])
        t1 = sb("t1", [P, TOK])
        hb = [sb(f"hb{i}", [P, TOK]) for i in range(2)]
        h_hi = [sb(f"h_hi{i}", [P, TOK], F16) for i in range(2)]
        h_lo = [sb(f"h_lo{i}", [P, TOK], F16) for i in range(2)]
        stats3 = sb("stats3", [P, 6])
        mv3 = sb("mv3", [P, 2])
        ve3 = sb("ve3", [P, 1])
        rstd3 = sb("rstd3", [P, 1])
        q = sb("q", [P, FEAT])
        q_hi = sb("q_hi", [P, FEAT], F32R)
        q_lo = sb("q_lo", [P, FEAT], F32R)
        qz = [sb(f"qz{i}", [P, PAIRS, 2 * FEAT], F32R) for i in range(2)]
        ks = [sb(f"ks{i}", [P, PAIRS, FEAT], F32R) for i in range(2)]
        v_hi = sb("v_hi", [P, HALF, HEADS, CH + 1], F16)
        v_lo = sb("v_lo", [P, HALF, HEADS, CH + 1], F16)
        mx = sb("mx", [P, HALF, HEADS])
        shift = sb("shift", [HEADS, FEAT], F32R)
        pr = [sb(f"pr{i}", [P, 2 * FEAT]) for i in range(2)]
        pr_hi = [sb(f"pr_hi{i}", [P, 2 * FEAT], F16) for i in range(4)]
        pr_lo = [sb(f"pr_lo{i}", [P, 2 * FEAT], F16) for i in range(4)]
        rsum = sb("rsum", [P, HALF * HEADS])
        att = sb("att", [P, HALF, POS])
        stats4 = sb("stats4", [P, 6])
        mv4 = sb("mv4", [P, 2])
        ve4 = sb("ve4", [P, 1])
        rstd4 = sb("rstd4", [P, 1])
        x4n = sb("x4n", [P, FEAT])
        x4T = sb("x4T", [P, HALF, POS])
        fo = sb("fo", [P, FEAT])
        sc = sb("sc", [P, 12])

        gate_ps, up_ps = bank("gate_ps"), bank("up_ps")
        y_ps = [bank("y_ps0"), bank("y_ps1")]
        score_ps = [bank("score_ps0"), bank("score_ps1")]
        av_ps, misc_ps = bank("av_ps"), bank("misc_ps")
        av = av_ps[:, 0:HALF * HEADS * (CH + 1)].rearrange("p (g c) -> p g c", c=CH + 1)

        def sem(name):
            return ctx.enter_context(nc.semaphore(name))

        early_in = sem("early_in")
        consts_in = sem("consts_in")
        consts_set = sem("consts_set")
        gate_w_hi = sem("gate_w_hi")
        gate_w_lo = sem("gate_w_lo")
        x_in = sem("x_in")
        v_in = sem("v_in")
        var_ready = sem("var_ready")
        rstd_ready = sem("rstd_ready")
        xn_ready = sem("xn_ready")
        top_ready = sem("top_ready")
        own_ready = sem("own_ready")
        gaps_ready = sem("gaps_ready")
        exps_ready = sem("exps_ready")
        vs_ready = sem("vs_ready")
        yk_ready = sem("yk_ready")
        x2_hi_ready = sem("x2_hi_ready")
        dve_step = sem("dve_step")
        logits_exp = sem("logits_exp")
        w13_hi_ready = sem("w13_hi_ready")
        w13_lo_ready = sem("w13_lo_ready")
        w2_hi_ready = sem("w2_hi_ready")
        w2_lo_ready = sem("w2_lo_ready")
        gate_ready = sem("gate_ready")
        tanh_ready = sem("tanh_ready")
        gate_used = sem("gate_used")
        route_used = sem("route_used")
        route_set = sem("route_set")
        route_out = sem("route_out")
        route_in = [sem(f"route_in{i}") for i in range(3)]
        max_read = sem("max_read")
        exp_read = sem("exp_read")
        pr_hi_ready = sem("pr_hi_ready")
        pr_lo_ready = sem("pr_lo_ready")
        v_hi_ready = sem("v_hi_ready")
        att_ready = sem("att_ready")
        up_ready = sem("up_ready")
        h_ready = sem("h_ready")
        h_hi_ready = sem("h_hi_ready")
        h_lo_ready = sem("h_lo_ready")
        y_done = sem("y_done")
        y_copied = sem("y_copied")
        y_turned = sem("y_turned")
        y_added = sem("y_added")
        var3_ready = sem("var3_ready")
        rstd3_ready = sem("rstd3_ready")
        q_ready = sem("q_ready")
        q_hi_ready = sem("q_hi_ready")
        q_lo_ready = sem("q_lo_ready")
        kraw_in = sem("kraw_in")
        ks_hi_ready = sem("ks_hi_ready")
        ks_ready = sem("ks_ready")
        vb_in = sem("vb_in")
        v_ready = sem("v_ready")
        q_out0 = sem("q_out0")
        q_out1 = sem("q_out1")
        qz_in0 = sem("qz_in0")
        qz_in1 = sem("qz_in1")
        shift_out = sem("shift_out")
        shift_in = sem("shift_in")
        score_written = sem("score_written")
        av_done = sem("av_done")
        var4_ready = sem("var4_ready")
        rstd4_ready = sem("rstd4_ready")
        x4_ready = sem("x4_ready")
        misc_written = sem("misc_written")
        misc_read = sem("misc_read")
        square_ready = sem("square_ready")
        norm_ready = sem("norm_ready")
        norm1_ready = sem("norm1_ready")
        tanh1_ready = sem("tanh1_ready")
        res_ready = sem("res_ready")
        stored = sem("stored")
        stage_in = [sem(f"stage_in{i}") for i in range(3)]
        q_out = [q_out0, q_out1]
        qz_in = [qz_in0, qz_in1]

        N_EARLY = 3
        N_CONSTS = 2
        N_SET = 12

        block = ctx.enter_context(nc.Block())

        @block.sync
        def _(sp):
            def load_const(dst, src):
                sp.dma_start(dst, src).then_inc(consts_in, 16)

            sp.dma_start(wu[:, :, :], decay_bonus).then_inc(early_in, 16)
            sp.dma_start(eye_sb[:, :], eye).then_inc(early_in, 16)
            sp.dma_start(gw[:, :, :], gate_w).then_inc(early_in, 16)

            def load(n):
                sp.dma_start(res[n][:, :, :], x[BB * n:BB * n + BB].rearrange("b t c -> t b c")).then_inc(x_in, 16)
                if n >= 1:
                    sp.wait_ge(v_in, 32 * n)
                    sp.wait_ge(vs_ready, 4 * n)
                for h in range(HALF):
                    sp.dma_start(vT[:, h, :, :], ctx_feat[BB * n:BB * n + BB, h * P:(h + 1) * P, :].rearrange("b p t -> p b t")).then_inc(v_in, 16)
                if n == 0:
                    load_const(ffn_sb[:, :, :], ffn_w)
                    load_const(ffn_s[:, :], ffn_scale.partition_broadcast(P))


            def wkv(n, w):
                if w == 0:
                    load(n)
                if w == ROUTE + 1:
                    sp.wait_ge(misc_read, misc_no[("route", n)])
                    if n >= 1:
                        sp.wait_ge(route_out, 16 * n)
                    if n >= 2:
                        for i in range(3):
                            last = max(r for r in range(ROUTED * (n - 1)) if r % 3 == i)
                            sp.wait_ge(route_in[i], parts_in[last])
                    sp.dma_start(c_scratch[n % 2], cT[:, :]).then_inc(route_out, 16)

            def route(slot):
                t = (slot + 3) // 3
                n, j = t // TILES, t % TILES
                if slot % 3 == 0 and 0 <= t < TILES * BLOCKS and j < ROUTED:
                    r = ROUTED * n + j
                    if j == 0:
                        sp.wait_ge(route_out, 16 * (n + 1))
                    if r >= 3:
                        sp.wait_ge(route_used, r - 2)
                        sp.wait_ge(route_in[r % 3], parts_in[r - 3])
                    for e, a, b in parts[r]:
                        sp.dma_start(cb[r % 3][a:b, :], c_scratch[n % 2, e].partition_broadcast(b - a)).then_inc(route_in[r % 3], 16)

            def weights(slot):
                if slot % 3 == 0 and 0 <= slot // 3 + 5 < TILES:
                    j = slot // 3 + 5
                    if j >= 3:
                        sp.wait_ge(w13_hi_ready, j - 2)
                        sp.wait_ge(w13_lo_ready, j - 2)
                        sp.wait_ge(w2_lo_ready, j - 2)
                        sp.wait_ge(stage_in[j % 3], 16 * (j // 3))
                    sp.dma_start(stage[j % 3], experts[j]).then_inc(stage_in[j % 3], 16)

            def attention(m, a):
                i = m % 2
                if a == 0:
                    if m >= 1:
                        sp.wait_ge(ks_ready, m)
                        sp.wait_ge(v_ready, m)
                        sp.wait_ge(kraw_in, 16 * m)
                        sp.wait_ge(vb_in, 16 * m)
                    else:
                        sp.wait_ge(w2_lo_ready, TILES)
                        for i in range(3):
                            sp.wait_ge(stage_in[i], 16 * len(range(i, TILES, 3)))
                    sp.dma_start(kraw, ctx_heads[m]).then_inc(kraw_in, 16)
                    sp.dma_start(vb, ctx_feat[m].rearrange("(h p) t -> p h t", p=P)).then_inc(vb_in, 16)
                if a == 2:
                    sp.wait_ge(q_hi_ready, m + 1)
                    if m >= 2:
                        sp.wait_ge(qz_in[i], 96 * (m // 2))
                    sp.dma_start(q_scratch[i, 0], q_hi[:, :].bitcast(F32)).then_inc(q_out[i], 16)
                    sp.wait_ge(q_lo_ready, m + 1)
                    sp.dma_start(q_scratch[i, 1], q_lo[:, :].bitcast(F32)).then_inc(q_out[i], 16)
                if a == 4:
                    sp.wait_ge(q_out[i], 32 * (m // 2 + 1))
                    if m >= 2:
                        sp.wait_ge(score_written, score_no[("exp", m - 2, 7)])
                    for row, part, head, col in ((0, 0, 0, 0), (16, 1, 0, 0), (64, 0, 0, 0),
                                                 (32, 0, 4, FEAT), (48, 1, 4, FEAT), (80, 0, 4, FEAT)):
                        src = q_scratch[i, part, head * CH:(head + PAIRS) * CH, :].rearrange("(p c) t -> c p t", c=CH)
                        sp.dma_start(qz[i][row:row + CH, :, col:col + FEAT].bitcast(F32), src).then_inc(qz_in[i], 16)
                if a == SHIFT + 1:
                    sp.wait_ge(misc_read, misc_no[("shift", m)])
                    if m >= 2:
                        sp.wait_ge(shift_in, 32 * (m - 1))
                    sp.dma_start(m_scratch[i], shift[:, :].bitcast(F32)).then_inc(shift_out, 16)
                    sp.wait_ge(shift_out, 16 * (m + 1))
                    for half in range(2):
                        sp.dma_start(qz[i][STACK + half:STACK + half + 1, :, half * FEAT:(half + 1) * FEAT].bitcast(F32),
                                     m_scratch[i:i + 1, half * PAIRS:(half + 1) * PAIRS, :]).then_inc(shift_in, 16)
                if a == ATTN_LAST:
                    sp.wait_ge(res_ready, m + 1)
                    sp.dma_start(out[m], res[m // BB][:, m % BB, :]).then_inc(stored, 16)

            for slot in range(FIRST_SLOT, LAST_SLOT + 1):
                weights(slot)
                route(slot)
                for m, a in attn_steps(slot):
                    attention(m, a)
                for n, w in wkv_steps(slot):
                    wkv(n, w)
            sp.wait_ge(stored, 16 * BATCH)

        @block.gpsimd
        def _(pool):
            nc.gpsimd.memset(neg_half[:, :], -0.5).then_inc(consts_set, 1)
            nc.gpsimd.memset(pos_half[:, :], 0.5).then_inc(consts_set, 1)
            nc.gpsimd.memset(top[:, :, 0:1], NEG).then_inc(consts_set, 1)
            nc.gpsimd.memset(num_s[:, :, 0:1], 0.0).then_inc(consts_set, 1)
            nc.gpsimd.memset(den_s[:, :, 0:1], 0.0).then_inc(consts_set, 1)
            nc.gpsimd.memset(probs[:, :, EXPERTS:EXPERTS + 2], 3.0).then_inc(consts_set, 1)
            nc.gpsimd.memset(v_hi[:, :, :, CH:CH + 1], 1.0).then_inc(consts_set, 1)
            nc.gpsimd.memset(v_lo[:, :, :, CH:CH + 1], 0.0).then_inc(consts_set, 1)
            for i in range(2):
                nc.gpsimd.memset(qz[i][:, :, :].bitcast(F32), 0.0).then_inc(consts_set, 1)
            pool.wait_ge(consts_set, N_SET)
            def norm_scale(var_ready, no, dst, src, width, rstd_ready):
                pool.wait_ge(var_ready, no)
                nc.gpsimd.tensor_tensor(dst, src, neg_half[:, 0:width], ALU.pow).then_inc(rstd_ready, 1)

            def moe(slot):
                t, r = slot // 3, slot % 3
                if r == 2 and 0 <= t < TILES * BLOCKS:
                    pool.wait_ge(h_hi_ready, t + 1)
                    nc.gpsimd.tensor_tensor(h_lo[t % 2][:, :], hb[t % 2][:, :], h_hi[t % 2][:, :],
                                            ALU.subtract).then_inc(h_lo_ready, 1)

            def weights(slot):
                if slot % 3 == 0 and 0 <= slot // 3 + 3 < TILES:
                    j = slot // 3 + 3
                    pool.wait_ge(w2_hi_ready, j + 1)
                    pool.wait_ge(w13_lo_ready, j + 1)
                    nc.gpsimd.tensor_tensor(w2_lo[:, j, :], stage[j % 3][:, 2 * FEAT:3 * FEAT], w2_hi[:, j, :],
                                            ALU.subtract).then_inc(w2_lo_ready, 1)

            def attention(m, a):
                i = m % 2
                if a == 0:
                    norm_scale(var3_ready, m + 1, rstd3[:, :], ve3[:, :], 1, rstd3_ready)
                if a == 1:
                    pool.wait_ge(q_hi_ready, m + 1)
                    if m >= 1:
                        pool.wait_ge(q_out[(m - 1) % 2], 32 * ((m - 1) // 2 + 1))
                    nc.gpsimd.tensor_tensor(q_lo[:, :], q[:, :], q_hi[:, :].bitcast(F32), ALU.subtract).then_inc(q_lo_ready, 1)
                if a == V_SPLIT:
                    pool.wait_ge(v_hi_ready, 2 * (m + 1))
                    for st in range(HALF):
                        ins = nc.gpsimd.tensor_tensor(v_lo[:, st, :, 0:CH], vb[:, st, :].rearrange("p (h c) -> p h c", h=HEADS),
                                                      v_hi[:, st, :, 0:CH], ALU.subtract)
                    ins.then_inc(v_ready, 1)
                if EXPS + 1 <= a < EXPS + 9:
                    e = a - EXPS - 1
                    pool.wait_ge(pr_hi_ready, 8 * m + e + 1)
                    if 8 * m + e >= 4:
                        pool.wait_ge(av_done, 8 * m + e - 3)
                    nc.gpsimd.tensor_tensor(pr_lo[e % 4][:, :], pr[e % 2][:, :], pr_hi[e % 4][:, :],
                                            ALU.subtract).then_inc(pr_lo_ready, 1)
                if a == ATT_TURN + 1:
                    norm_scale(var4_ready, m + 1, rstd4[:, :], ve4[:, :], 1, rstd4_ready)
                if a == FFN + 2:
                    pool.wait_ge(square_ready, m + 1)
                    nc.gpsimd.tensor_tensor(sc[:, 1:2], sc[:, 0:1], pos_half[:, :], ALU.pow).then_inc(norm_ready, 1)

            def wkv(n, w):
                if w == 0:
                    norm_scale(var_ready, 2 * n + 1, rstd[:, :], ve[:, :], BB, rstd_ready)
                if w == X2_NORM:
                    norm_scale(var_ready, 2 * n + 2, rstd[:, :], ve[:, :], BB, rstd_ready)
                for h in range(HALF):
                    c = 2 * n + h
                    if w == HALVES + 1 + HALF_GAP * h:
                        pool.wait_ge(top_ready, c + 1)
                        nc.gpsimd.tensor_tensor(keep[:, :, :], top[:, :, 0:POS], top[:, :, 1:POS + 1],
                                                ALU.subtract).then_inc(gaps_ready, 1)
                        nc.gpsimd.tensor_tensor(take[:, :, :], kT[h][:, :, :], top[:, :, 1:POS + 1],
                                                ALU.subtract).then_inc(gaps_ready, 1)
                    if w == HALVES + 3 + HALF_GAP * h:
                        if c == 0:
                            pool.wait_ge(v_in, 32)
                        elif h == 0:
                            pool.wait_ge(v_in, 32 * (n + 1))
                        if c >= 1:
                            pool.wait_ge(misc_written, misc_no[("y", (c - 1) // 2, (c - 1) % 2)])
                        pool.wait_ge(exps_ready, 3 * c + 3)
                        nc.gpsimd.tensor_tensor(take_v[:, :, :], take[:, :, :], vT[:, h, :, :], ALU.mult).then_inc(vs_ready, 1)
                        nc.gpsimd.tensor_tensor(now_v[:, :, :], now[:, :, :], vT[:, h, :, :], ALU.mult).then_inc(vs_ready, 1)

            for slot in range(FIRST_SLOT, LAST_SLOT + 1):
                moe(slot)
                weights(slot)
                for m, a in attn_steps(slot):
                    attention(m, a)
                for n, w in wkv_steps(slot):
                    wkv(n, w)

        @block.scalar
        def _(act):
            def moe(slot):
                t, r = slot // 3, slot % 3
                if 0 <= t < TILES * BLOCKS:
                    if r == 0:
                        act.wait_ge(gate_ready, t + 1)
                        if t >= 1:
                            act.wait_ge(gate_used, t)
                        nc.scalar.activation(th[:, :], gate_ps[:, :], ACT.Tanh, scale=0.5 / W_SCALE).then_inc(tanh_ready, 1)
                    if r == 2:
                        act.wait_ge(h_ready, t + 1)
                        if t >= 2:
                            act.wait_ge(y_done, t - 1)
                        nc.scalar.activation(h_hi[t % 2][:, :], hb[t % 2][:, :], ACT.Copy).then_inc(h_hi_ready, 1)
                n = slot // SLOTS - 1
                if 0 <= n < BLOCKS and slot % SLOTS == 2:
                    act.wait_ge(y_done, TILES * (n + 1))
                    if n >= 1:
                        act.wait_ge(y_turned, n)
                    for c in range(HALF):
                        nc.scalar.activation(ysb[:, c, :], y_ps[c][:, :], ACT.Copy,
                                             scale=1.0 / (H_SCALE * W_SCALE)).then_inc(y_copied, 1)

            def weights(slot):
                if slot % 3 == 0 and 0 <= slot // 3 + 3 < TILES:
                    j = slot // 3 + 3
                    act.wait_ge(stage_in[j % 3], 16 * (j // 3 + 1))
                    nc.scalar.activation(w13_hi[:, j, :, :, :].rearrange("p a b c -> p (a b c)"),
                                         stage[j % 3][:, 0:2 * FEAT], ACT.Copy, scale=W_SCALE).then_inc(w13_hi_ready, 1)
                    act.wait_ge(w13_lo_ready, j + 1)
                    nc.scalar.activation(w2_hi[:, j, :], stage[j % 3][:, 2 * FEAT:3 * FEAT], ACT.Copy).then_inc(w2_hi_ready, 1)

            def attention(m, a):
                i = m % 2
                if a == 1:
                    act.wait_ge(q_ready, m + 1)
                    if m >= 1:
                        act.wait_ge(q_out[(m - 1) % 2], 32 * ((m - 1) // 2 + 1))
                    nc.scalar.activation(q_hi[:, :], q[:, :], ACT.Copy).then_inc(q_hi_ready, 1)
                if a == 2:
                    act.wait_ge(kraw_in, 16 * (m + 1))
                    if m >= 2:
                        act.wait_ge(score_written, score_no[("exp", m - 2, 7)])
                    nc.scalar.activation(ks[i][0:STACK, :, :], kraw, ACT.Copy).then_inc(ks_hi_ready, 1)
                if a == SHIFT:
                    act.wait_ge(misc_written, misc_no[("shift", m)])
                    if m >= 1:
                        act.wait_ge(shift_out, 16 * m)
                    nc.scalar.activation(shift[:, :], misc_ps[0:HEADS, 0:FEAT], ACT.Copy, scale=-1.0).then_inc(misc_read, 1)
                if EXPS <= a < EXPS + 8:
                    e = a - EXPS
                    no = score_no[("exp", m, e)]
                    act.wait_ge(score_written, no)
                    if 8 * m + e >= 2:
                        act.wait_ge(pr_lo_ready, 8 * m + e - 1)
                    nc.scalar.activation(pr[e % 2][:, :], score_ps[no % 2][:, :], ACT.Exp, scale=1.0 / CH).then_inc(exp_read, 1)
                    act.wait_ge(exp_read, 8 * m + e + 1)
                    if 8 * m + e >= 4:
                        act.wait_ge(av_done, 8 * m + e - 3)
                    nc.scalar.activation(pr_hi[e % 4][:, :], pr[e % 2][:, :], ACT.Copy).then_inc(pr_hi_ready, 1)
                if a == V_SPLIT:
                    act.wait_ge(vb_in, 16 * (m + 1))
                    if m >= 1:
                        act.wait_ge(av_done, 8 * m)
                    for st in range(HALF):
                        nc.scalar.activation(v_hi[:, st, :, 0:CH], vb[:, st, :].rearrange("p (h c) -> p h c", h=HEADS),
                                             ACT.Copy).then_inc(v_hi_ready, 1)
                if a == X4_TURN:
                    act.wait_ge(misc_written, misc_no[("x4", m)])
                    nc.scalar.activation(x4T[:, :, :], misc_ps[:, 0:FEAT].rearrange("p (h t) -> p h t", h=HALF),
                                         ACT.Copy).then_inc(misc_read, 1)
                if a == FFN + 3:
                    act.wait_ge(norm1_ready, m + 1)
                    nc.scalar.activation(sc[:, 3:4], sc[:, 2:3], ACT.Tanh).then_inc(tanh1_ready, 1)

            def wkv(n, w):
                for h in range(HALF):
                    c = 2 * n + h
                    if w == K_TURN + h:
                        act.wait_ge(misc_written, misc_no[("k", n, h)])
                        nc.scalar.activation(kT[h][:, :, :], misc_ps[:, :].rearrange("p (b t) -> p b t", b=BB),
                                             ACT.Copy).then_inc(misc_read, 1)
                    if w == HALVES + 2 + HALF_GAP * h:
                        if c == 0:
                            act.wait_ge(early_in, 16 * N_EARLY)
                        act.wait_ge(gaps_ready, 2 * c + 2)
                        nc.scalar.activation(keep[:, :, :], keep[:, :, :], ACT.Exp, bias=wu[:, h, 0:1]).then_inc(exps_ready, 1)
                        nc.scalar.activation(take[:, :, :], take[:, :, :], ACT.Exp).then_inc(exps_ready, 1)
                        act.wait_ge(own_ready, c + 1)
                        nc.scalar.activation(now[:, :, :], now[:, :, :], ACT.Exp).then_inc(exps_ready, 1)
                    if w == X2_TURN + 2 * h:
                        if n >= 2:
                            act.wait_ge(up_ready, TILES * (n - 1))
                        act.wait_ge(misc_written, misc_no[("x2", n, h)])
                        nc.scalar.activation(xT_hi[n % 2][:, h, :], misc_ps[:, :], ACT.Copy).then_inc(x2_hi_ready, 1)
                if w == GATE:
                    act.wait_ge(misc_read, misc_no[("gate", n)])
                    nc.scalar.activation(ex[:, :, :], lg[:, :, :], ACT.Exp, scale=1.0 / W_SCALE).then_inc(logits_exp, 1)
                if w == ROUTE:
                    act.wait_ge(misc_written, misc_no[("route", n)])
                    if n >= 1:
                        act.wait_ge(route_out, 16 * n)
                    nc.scalar.activation(cT[:, :], misc_ps[0:EXPERTS, :], ACT.Copy).then_inc(misc_read, 1)

            act.wait_ge(early_in, 16 * N_EARLY)
            nc.scalar.activation(gw_hi[:, :, :], gw[:, :, :], ACT.Copy, scale=W_SCALE).then_inc(gate_w_hi, 1)
            for slot in range(FIRST_SLOT, LAST_SLOT + 1):
                moe(slot)
                weights(slot)
                for m, a in attn_steps(slot):
                    attention(m, a)
                for n, w in wkv_steps(slot):
                    wkv(n, w)

        @block.vector
        def _(dve):
            steps = [0]

            def link(ins):
                steps[0] += 1
                ins.then_inc(dve_step, 1)
                dve.wait_ge(dve_step, steps[0])

            def norm_stats(xs, st, mean_var, var_eps, var_ready):
                for b, xb in enumerate(xs):
                    ins = nc.vector.bn_stats(st[b], xb)
                link(ins)
                for b in range(len(xs)):
                    ins = nc.vector.bn_aggr(mean_var[b], st[b])
                link(ins)
                nc.vector.tensor_scalar(var_eps[0], var_eps[1], LN_EPS, None, ALU.add).then_inc(var_ready, 1)

            def moe(slot):
                t, r = slot // 3, slot % 3
                if 0 <= t < TILES * BLOCKS:
                    if r == 0:
                        dve.wait_ge(tanh_ready, t + 1)
                        nc.vector.scalar_tensor_tensor(t1[:, :], th[:, :], 1.0, gate_ps[:, :], ALU.add,
                                                       ALU.mult).then_inc(gate_used, 1)
                    if r == 1:
                        j = t % TILES
                        dve.wait_ge(gate_used, t + 1)
                        if j < ROUTED:
                            c = ROUTED * (t // TILES) + j
                            dve.wait_ge(route_in[c % 3], parts_in[c])
                            nc.vector.tensor_tensor(t1[:, :], t1[:, :], cb[c % 3][:, :], ALU.mult).then_inc(route_used, 1)
                            dve.wait_ge(route_used, c + 1)
                        dve.wait_ge(up_ready, t + 1)
                        if t >= 2:
                            dve.wait_ge(h_lo_ready, t - 1)
                        if j < ROUTED:
                            nc.vector.tensor_tensor(hb[t % 2][:, :], t1[:, :], up_ps[:, :], ALU.mult).then_inc(h_ready, 1)
                        else:
                            nc.vector.scalar_tensor_tensor(hb[t % 2][:, :], t1[:, :], ROUTE_SCALE, up_ps[:, :], ALU.mult,
                                                           ALU.mult).then_inc(h_ready, 1)
                n = slot // SLOTS - 1
                if 0 <= n < BLOCKS and slot % SLOTS == 4:
                    dve.wait_ge(y_turned, n + 1)
                    for c in range(2):
                        part = res[n][:, 2 * c:2 * c + 2, :]
                        ins = nc.vector.tensor_tensor(part, part, y_ps[c][:, :].rearrange("p (b f) -> p b f", b=2), ALU.add)
                    ins.then_inc(y_added, 1)
                    dve.wait_ge(y_added, n + 1)

            def weights(slot):
                if slot % 3 == 0 and 0 <= slot // 3 + 3 < TILES:
                    j = slot // 3 + 3
                    dve.wait_ge(stage_in[j % 3], 16 * (j // 3 + 1))
                    part = stage[j % 3][:, 2 * FEAT:3 * FEAT]
                    nc.vector.tensor_scalar(part, part, W_SCALE, None, ALU.mult)
                    dve.wait_ge(w13_hi_ready, j + 1)
                    nc.vector.scalar_tensor_tensor(w13_lo[:, j, :, :, :].rearrange("p a b c -> p (a b c)"),
                                                   stage[j % 3][:, 0:2 * FEAT], W_SCALE,
                                                   w13_hi[:, j, :, :, :].rearrange("p a b c -> p (a b c)"),
                                                   ALU.mult, ALU.subtract).then_inc(w13_lo_ready, 1)

            def attention(m, a):
                xb = res[m // BB][:, m % BB, :]
                if a == 0:
                    norm_stats([xb], [stats3[:, :]], [mv3[:, :]], (ve3[:, :], mv3[:, 1:2]), var3_ready)
                if a == 1:
                    dve.wait_ge(rstd3_ready, m + 1)
                    if m >= 1:
                        dve.wait_ge(q_lo_ready, m)
                    nc.vector.tensor_scalar(q[:, :], xb, mv3[:, 0:1], rstd3[:, 0:1], ALU.subtract, ALU.mult).then_inc(q_ready, 1)
                if a == 3:
                    dve.wait_ge(ks_hi_ready, m + 1)
                    low = ks[m % 2][64:STACK, :, :]
                    nc.vector.tensor_tensor(low, kraw[64:STACK, :, :], low.bitcast(F32), ALU.subtract).then_inc(ks_ready, 1)
                if MAXIMA <= a < MAXIMA + 8:
                    v = a - MAXIMA
                    p, tt = v // 2, v % 2
                    no = score_no[("max", m, v)]
                    dve.wait_ge(score_written, no)
                    dst = mx[:, tt, :].rearrange("q (a p) -> q a p", a=2)[:, :, p]
                    nc.vector.tensor_reduce(dst, score_ps[no % 2][:, :].rearrange("q (a k) -> q a k", a=2), AX_X,
                                            ALU.max).then_inc(max_read, 1)
                if a == VALUES_OUT:
                    dve.wait_ge(av_done, 8 * (m + 1))
                    link(nc.vector.reciprocal(rsum[:, :], av[:, :, CH]))
                    if m >= 1:
                        dve.wait_ge(misc_written, misc_no[("att", m - 1)])
                    nc.vector.tensor_tensor(att[:, :, :].rearrange("p t (h c) -> p (t h) c", h=HEADS), av[:, :, 0:CH],
                                            rsum[:, :].unsqueeze(2).to_broadcast([P, HALF * HEADS, CH]), ALU.mult).then_inc(att_ready, 1)
                if a == ATT_TURN:
                    dve.wait_ge(misc_written, misc_no[("att", m)])
                    nc.vector.tensor_tensor(xb, xb, misc_ps[:, 0:FEAT], ALU.add).then_inc(misc_read, 1)
                    dve.wait_ge(misc_read, misc_no[("att", m)])
                if a == ATT_TURN + 1:
                    norm_stats([xb], [stats4[:, :]], [mv4[:, :]], (ve4[:, :], mv4[:, 1:2]), var4_ready)
                if a == ATT_TURN + 2:
                    dve.wait_ge(rstd4_ready, m + 1)
                    nc.vector.tensor_scalar(x4n[:, :], xb, mv4[:, 0:1], rstd4[:, 0:1], ALU.subtract, ALU.mult).then_inc(x4_ready, 1)
                if a == FFN:
                    dve.wait_ge(misc_written, misc_no[("ffn", m)])
                    if m == 0:
                        dve.wait_ge(consts_in, 16 * N_CONSTS)
                    nc.vector.tensor_tensor(fo[:, :], misc_ps[:, 0:FEAT], ffn_s[:, :], ALU.mult).then_inc(misc_read, 1)
                    dve.wait_ge(misc_read, misc_no[("ffn", m)])
                    nc.vector.tensor_tensor_reduce(x4n[:, :], fo[:, :], fo[:, :], 1.0, 0.0, ALU.mult, ALU.add,
                                                   sc[:, 0:1]).then_inc(square_ready, 1)
                if a == FFN + 2:
                    dve.wait_ge(norm_ready, m + 1)
                    nc.vector.tensor_scalar(sc[:, 2:3], sc[:, 1:2], BALL_EPS, None, ALU.max).then_inc(norm1_ready, 1)
                    dve.wait_ge(norm1_ready, m + 1)
                    link(nc.vector.tensor_scalar(sc[:, 4:5], sc[:, 2:3], BALL_EPS, None, ALU.add))
                    link(nc.vector.reciprocal(sc[:, 5:6], sc[:, 4:5]))
                if a == FFN + 4:
                    dve.wait_ge(tanh1_ready, m + 1)
                    link(nc.vector.tensor_tensor(sc[:, 6:7], sc[:, 3:4], sc[:, 5:6], ALU.mult))
                    link(nc.vector.tensor_tensor(sc[:, 7:8], sc[:, 1:2], sc[:, 6:7], ALU.mult))
                    link(nc.vector.tensor_scalar(sc[:, 8:9], sc[:, 7:8], BALL_EPS, None, ALU.max))
                    link(nc.vector.reciprocal(sc[:, 9:10], sc[:, 8:9]))
                    link(nc.vector.tensor_scalar(sc[:, 10:11], sc[:, 9:10], MAX_NORM, 1.0, ALU.mult, ALU.min))
                    link(nc.vector.tensor_tensor(sc[:, 11:12], sc[:, 10:11], sc[:, 6:7], ALU.mult))
                    nc.vector.scalar_tensor_tensor(xb, fo[:, :], sc[:, 11:12], xb, ALU.mult, ALU.add).then_inc(res_ready, 1)

            def block_norm(n, k):
                r = res[n]
                norm_stats([r[:, b, :] for b in range(BB)], [stats[:, b, :] for b in range(BB)],
                           [mv[:, b, :] for b in range(BB)], (ve[:, :], mv[:, :, 1]), var_ready)

            def block_normed(n, k):
                dve.wait_ge(rstd_ready, 2 * n + k + 1)
                for b in range(BB):
                    ins = nc.vector.tensor_scalar(xn[:, b, :], res[n][:, b, :], mv[:, b, 0:1], rstd[:, b:b + 1],
                                                  ALU.subtract, ALU.mult)
                ins.then_inc(xn_ready, 1)

            def wkv(n, w):
                if w == 0:
                    dve.wait_ge(x_in, 16 * (n + 1))
                    block_norm(n, 0)
                if w == 1:
                    if n >= 1:
                        dve.wait_ge(misc_written, misc_no[("x2", n - 1, 1)])
                    block_normed(n, 0)
                for h in range(HALF):
                    c = 2 * n + h
                    u = w - HALVES - HALF_GAP * h
                    if u == 0:
                        if c == 0:
                            dve.wait_ge(early_in, 16 * N_EARLY)
                            dve.wait_ge(consts_set, N_SET)
                        dve.wait_ge(misc_read, misc_no[("k", n, h)])
                        for b in range(BB):
                            ins = nc.vector.tensor_tensor_scan(top[:, b, 1:POS + 1], wu[:, h, 0:1].to_broadcast([P, POS]),
                                                               kT[h][:, b, :], NEG, ALU.add, ALU.max)
                        ins.then_inc(top_ready, 1)
                        dve.wait_ge(top_ready, c + 1)
                    if u == 1:
                        link(nc.vector.scalar_tensor_tensor(now[:, :, :], kT[h][:, :, :], wu[:, h, 1:2], top[:, :, 0:POS],
                                                            ALU.add, ALU.subtract))
                        nc.vector.tensor_scalar(now[:, :, :], now[:, :, :], CLAMP, None, ALU.min).then_inc(own_ready, 1)
                    if u == 3:
                        dve.wait_ge(exps_ready, 3 * c + 3)
                        for b in range(BB):
                            nc.vector.tensor_tensor_scan(den_s[:, b, 1:POS + 1], keep[:, b, :], take[:, b, :], 0.0,
                                                         ALU.mult, ALU.add)
                    if u == 5:
                        dve.wait_ge(vs_ready, 2 * c + 2)
                        for b in range(BB):
                            ins = nc.vector.tensor_tensor_scan(num_s[:, b, 1:POS + 1], keep[:, b, :], take_v[:, b, :], 0.0,
                                                               ALU.mult, ALU.add)
                        link(ins)
                    if u == 6:
                        if c >= 1:
                            dve.wait_ge(misc_written, misc_no[("y", (c - 1) // 2, (c - 1) % 2)])
                        nc.vector.tensor_tensor(yk[:, :, :], num_s[:, :, 0:POS], now_v[:, :, :], ALU.add)
                        link(nc.vector.tensor_tensor(now[:, :, :], den_s[:, :, 0:POS], now[:, :, :], ALU.add))
                    if u in (8, 9):
                        lo = 2 * (u - 8)
                        link(nc.vector.reciprocal(now[:, lo:lo + 2, :], now[:, lo:lo + 2, :]))
                    if u == 11:
                        nc.vector.tensor_tensor(yk[:, :, :], yk[:, :, :], now[:, :, :], ALU.mult).then_inc(yk_ready, 1)
                    if u == Y_TURN:
                        dve.wait_ge(misc_written, misc_no[("y", n, h)])
                        part = res[n][:, :, h * P:(h + 1) * P]
                        nc.vector.tensor_tensor(part, part, misc_ps[:, :].rearrange("p (b f) -> p b f", b=BB),
                                                ALU.add).then_inc(misc_read, 1)
                if w == X2_NORM:
                    dve.wait_ge(misc_read, misc_no[("y", n, 1)])
                    block_norm(n, 1)
                if w == X2_NORM + 1:
                    block_normed(n, 1)
                for h in range(HALF):
                    if w == X2_TURN + 2 * h:
                        dve.wait_ge(x2_hi_ready, 2 * n + h + 1)
                        nc.vector.tensor_tensor(xT_lo[n % 2][:, h, :], misc_ps[:, :], xT_hi[n % 2][:, h, :],
                                                ALU.subtract).then_inc(misc_read, 1)
                if w == GATE:
                    dve.wait_ge(misc_written, misc_no[("gate", n)])
                    logits = misc_ps[:, 0:BB * EXPERTS].rearrange("p (b e) -> p b e", b=BB)
                    link(nc.vector.tensor_reduce(lmax[:, :], logits, AX_X, ALU.max))
                    nc.vector.tensor_tensor(lg[:, :, :], logits, lmax[:, :].unsqueeze(2).to_broadcast([P, BB, EXPERTS]),
                                            ALU.subtract).then_inc(misc_read, 1)
                if w == TOP:
                    dve.wait_ge(logits_exp, n + 1)
                    link(nc.vector.tensor_reduce(small[:, 0, :], ex[:, :, :], AX_X, ALU.add))
                    link(nc.vector.reciprocal(small[:, 1, :], small[:, 0, :]))
                    link(nc.vector.tensor_tensor(probs[:, :, 0:EXPERTS], ex[:, :, :],
                                                 small[:, 1, :].unsqueeze(2).to_broadcast([P, BB, EXPERTS]), ALU.mult))
                if w == TOP + 1:
                    for b in range(BB):
                        ins = nc.vector.max(top8[:, b, :], probs[:, b, :])
                    link(ins)
                    for b in range(BB):
                        ins = nc.vector.match_replace(rest[:, b, :], top8[:, b, :], probs[:, b, :], 0.0)
                    link(ins)
                if w == TOP + 2:
                    if n >= 1:
                        dve.wait_ge(misc_written, misc_no[("route", n - 1)])
                    link(nc.vector.tensor_tensor(route[:, :, :], probs[:, :, 0:EXPERTS], rest[:, :, 0:EXPERTS], ALU.subtract))
                    link(nc.vector.tensor_reduce(small[:, 2, :], route[:, :, :], AX_X, ALU.add))
                    link(nc.vector.tensor_scalar(small[:, 2, :], small[:, 2, :], 1e-20, None, ALU.add))
                    link(nc.vector.reciprocal(small[:, 3, :], small[:, 2, :]))
                    link(nc.vector.tensor_scalar(small[:, 3, :], small[:, 3, :], ROUTE_SCALE, None, ALU.mult))
                    nc.vector.tensor_tensor(route[:, :, :], route[:, :, :],
                                            small[:, 3, :].unsqueeze(2).to_broadcast([P, BB, EXPERTS]), ALU.mult).then_inc(route_set, 1)

            for i in range(2):
                nc.vector.memset(ks[i][STACK:P, :, :].bitcast(F32), 1.0).then_inc(consts_set, 1)
            dve.wait_ge(gate_w_hi, 1)
            nc.vector.scalar_tensor_tensor(gw_lo[:, :, :], gw[:, :, :], W_SCALE, gw_hi[:, :, :], ALU.mult,
                                           ALU.subtract).then_inc(gate_w_lo, 1)
            for slot in range(FIRST_SLOT, LAST_SLOT + 1):
                moe(slot)
                weights(slot)
                for m, a in attn_steps(slot):
                    attention(m, a)
                for n, w in wkv_steps(slot):
                    wkv(n, w)

        @block.tensor
        def _(pe):
            def misc_free(key):
                if misc_no[key] > 1:
                    pe.wait_ge(misc_read, misc_no[key] - 1)

            def score_free(key):
                if score_no[key] > 2:
                    kind, m, u = score_of[score_no[key] - 2]
                    pe.wait_ge(max_read if kind == "max" else exp_read, 8 * m + u + 1)

            def rows(bank_ap, n, j, gu):
                i = n % 2
                for k in range(HALF):
                    for wt, xt in ((w13_hi, xT_hi), (w13_lo, xT_hi), (w13_hi, xT_lo)):
                        last = k == HALF - 1 and xt is xT_lo
                        ins = nc.tensor.matmul(bank_ap, wt[:, j, gu, k, :], xt[i][:, k, :],
                                               start=(k == 0 and wt is w13_hi and xt is xT_hi), stop=last)
                return ins

            def down(t):
                n, j = t // TILES, t % TILES
                pe.wait_ge(h_lo_ready, t + 1)
                if n == 0:
                    pe.wait_ge(w2_lo_ready, j + 1)
                elif j == 0:
                    pe.wait_ge(y_added, n)
                for c in range(HALF):
                    cols = slice(c * P, (c + 1) * P)
                    nc.tensor.matmul(y_ps[c][:, :], w2_hi[:, j, cols], h_hi[t % 2][:, :], start=(j == 0), stop=False)
                    nc.tensor.matmul(y_ps[c][:, :], w2_lo[:, j, cols], h_hi[t % 2][:, :], start=False, stop=False)
                    ins = nc.tensor.matmul(y_ps[c][:, :], w2_hi[:, j, cols], h_lo[t % 2][:, :], start=False,
                                           stop=(j == TILES - 1))
                ins.then_inc(y_done, 1)

            def moe(slot):
                t, r = slot // 3, slot % 3
                n, j = t // TILES, t % TILES
                if 0 <= t < TILES * BLOCKS:
                    if r == 0:
                        if j == 0:
                            pe.wait_ge(misc_read, misc_no[("x2", n, 1)])
                        if n == 0:
                            pe.wait_ge(w13_lo_ready, j + 1)
                        if t >= 1:
                            pe.wait_ge(gate_used, t)
                        rows(gate_ps[:, :], n, j, 0).then_inc(gate_ready, 1)
                    if r == 1:
                        if t >= 1:
                            pe.wait_ge(h_ready, t)
                        rows(up_ps[:, :], n, j, 1).then_inc(up_ready, 1)
                if r == 2 and 0 <= t - 1 < TILES * BLOCKS:
                    down(t - 1)
                b = slot // SLOTS - 1
                if 0 <= b < BLOCKS and slot % SLOTS == 4:
                    pe.wait_ge(y_copied, 2 * (b + 1))
                    for bb in range(BB):
                        for c in range(HALF):
                            col = (bb % 2) * FEAT + c * P
                            ins = nc.tensor.transpose(y_ps[bb // 2][:, col:col + P], ysb[:, c, bb * P:(bb + 1) * P], eye_sb[:, :])
                    ins.then_inc(y_turned, 1)

            def attention(m, a):
                i = m % 2
                if MAXIMA <= a < MAXIMA + 8:
                    v = a - MAXIMA
                    p, tt = v // 2, v % 2
                    if v == 0:
                        pe.wait_ge(qz_in[i], 96 * (m // 2 + 1))
                        pe.wait_ge(ks_ready, m + 1)
                    score_free(("max", m, v))
                    for half in range(2):
                        col = half * FEAT + tt * P
                        ins = nc.tensor.matmul(score_ps[score_no[("max", m, v)] % 2][:, half * FEAT:(half + 1) * FEAT], qz[i][0:STACK, p, col:col + P],
                                               ks[i][0:STACK, p, :], start=True, stop=True)
                    ins.then_inc(score_written, 1)
                if a == SHIFT:
                    misc_free(("shift", m))
                    pe.wait_ge(max_read, 8 * (m + 1))
                    for tt in range(HALF):
                        ins = nc.tensor.transpose(misc_ps[0:HEADS, tt * P:(tt + 1) * P], mx[:, tt, :], eye_sb[:, :])
                    ins.then_inc(misc_written, 1)
                if EXPS <= a < EXPS + 8:
                    e = a - EXPS
                    p, st = e // 2, e % 2
                    if e == 0:
                        pe.wait_ge(shift_in, 32 * (m + 1))
                    score_free(("exp", m, e))
                    nc.tensor.matmul(score_ps[score_no[("exp", m, e)] % 2][:, :], ks[i][0:STACK + 2, p, st * P:(st + 1) * P], qz[i][0:STACK + 2, p, :],
                                     start=True, stop=True).then_inc(score_written, 1)
                if VALUES <= a < VALUES + 8:
                    e = a - VALUES
                    p, st = e // 2, e % 2
                    if e == 0:
                        pe.wait_ge(v_ready, m + 1)
                        if m >= 1:
                            pe.wait_ge(att_ready, m)
                    pe.wait_ge(pr_lo_ready, 8 * m + e + 1)
                    for half in range(2):
                        h = p + PAIRS * half
                        for tt in range(HALF):
                            cols = slice(half * FEAT + tt * P, half * FEAT + (tt + 1) * P)
                            dst = av[:, tt * HEADS + h, :]
                            for pt, vt in ((pr_hi, v_hi), (pr_hi, v_lo), (pr_lo, v_hi)):
                                first = e == 0 and half == 0 and tt == 0 and pt is pr_hi and vt is v_hi
                                ins = nc.tensor.matmul(dst, pt[e % 4][:, cols], vt[:, st, h, :], start=first,
                                                       stop=(e == 7 and pt is pr_lo), skip_group_check=True)
                    ins.then_inc(av_done, 1)
                if a == ATT_TURN:
                    misc_free(("att", m))
                    pe.wait_ge(att_ready, m + 1)
                    for tt in range(HALF):
                        ins = nc.tensor.transpose(misc_ps[:, tt * P:(tt + 1) * P], att[:, tt, :], eye_sb[:, :])
                    ins.then_inc(misc_written, 1)
                if a == X4_TURN:
                    misc_free(("x4", m))
                    pe.wait_ge(x4_ready, m + 1)
                    for h in range(HALF):
                        ins = nc.tensor.transpose(misc_ps[:, h * P:(h + 1) * P], x4n[:, h * P:(h + 1) * P], eye_sb[:, :])
                    ins.then_inc(misc_written, 1)
                if a == FFN:
                    misc_free(("ffn", m))
                    pe.wait_ge(misc_read, misc_no[("x4", m)])
                    for h in range(HALF):
                        ins = nc.tensor.matmul(misc_ps[:, 0:FEAT], x4T[:, h, :], ffn_sb[:, h, :], start=(h == 0), stop=(h == HALF - 1))
                    ins.then_inc(misc_written, 1)

            def wkv(n, w):
                for h in range(HALF):
                    if w == K_TURN + h:
                        misc_free(("k", n, h))
                        pe.wait_ge(xn_ready, 2 * n + 1)
                        for b in range(BB):
                            ins = nc.tensor.transpose(misc_ps[:, b * P:(b + 1) * P], xn[:, b, h * P:(h + 1) * P], eye_sb[:, :])
                        ins.then_inc(misc_written, 1)
                    if w == HALVES + Y_TURN + HALF_GAP * h:
                        misc_free(("y", n, h))
                        pe.wait_ge(yk_ready, 2 * n + h + 1)
                        for b in range(BB):
                            ins = nc.tensor.transpose(misc_ps[:, b * P:(b + 1) * P], yk[:, b, :], eye_sb[:, :])
                        ins.then_inc(misc_written, 1)
                    if w == X2_TURN + 2 * h:
                        misc_free(("x2", n, h))
                        pe.wait_ge(xn_ready, 2 * n + 2)
                        for b in range(BB):
                            ins = nc.tensor.transpose(misc_ps[:, b * P:(b + 1) * P], xn[:, b, h * P:(h + 1) * P], eye_sb[:, :])
                        ins.then_inc(misc_written, 1)
                if w == GATE:
                    misc_free(("gate", n))
                    pe.wait_ge(gate_w_lo, 1)
                    i = n % 2
                    for b in range(BB):
                        for k in range(HALF):
                            tok = slice(b * P, (b + 1) * P)
                            for xt, wt in ((xT_hi, gw_hi), (xT_lo, gw_hi), (xT_hi, gw_lo)):
                                ins = nc.tensor.matmul(misc_ps[:, b * EXPERTS:(b + 1) * EXPERTS], xt[i][:, k, tok], wt[:, k, :],
                                                       start=(k == 0 and xt is xT_hi and wt is gw_hi),
                                                       stop=(k == HALF - 1 and wt is gw_lo))
                    ins.then_inc(misc_written, 1)
                if w == ROUTE:
                    misc_free(("route", n))
                    pe.wait_ge(route_set, n + 1)
                    for b in range(BB):
                        ins = nc.tensor.transpose(misc_ps[0:EXPERTS, b * P:(b + 1) * P], route[:, b, :], eye_sb[:, :])
                    ins.then_inc(misc_written, 1)

            pe.wait_ge(early_in, 16 * N_EARLY)
            pe.wait_ge(consts_in, 16 * N_CONSTS)
            pe.wait_ge(consts_set, N_SET)
            for slot in range(FIRST_SLOT, LAST_SLOT + 1):
                moe(slot)
                for m, a in attn_steps(slot):
                    attention(m, a)
                for n, w in wkv_steps(slot):
                    wkv(n, w)


def kernel(x, ctx_2048, L0_xattn_w, L0_xattn_u, L0_ffn_gate_w, L0_ffn_w13, L0_ffn_w2, L0_ffn_sw13, L0_ffn_sw2,
           L1_ffn_weight, L1_ffn_scale):
    import numpy as np
    import concourse.bacc as bacc
    from concourse.bass_utils import run_bass_kernel_spmd

    def arr(a):
        return np.asarray(a)

    x, c = arr(x), arr(ctx_2048)
    heads = c.reshape(BATCH, 2, PAIRS, CH, FEAT).transpose(0, 1, 3, 2, 4)
    a, b = heads[:, 0], heads[:, 1]
    ctx_heads = np.concatenate([a, a, b, b, a, b], axis=1)

    def inner(w):
        rows = np.concatenate([w, np.zeros((TILES * P - w.shape[0], FEAT), w.dtype)])
        return rows.reshape(TILES, P, HALF, P).transpose(0, 3, 2, 1)

    w13, sw13 = arr(L0_ffn_w13), arr(L0_ffn_sw13)
    gate = inner(np.concatenate([w13[:, :INNER].reshape(-1, FEAT), sw13[:SHARED]]))
    up = inner(np.concatenate([w13[:, INNER:].reshape(-1, FEAT), sw13[SHARED:]]))
    w2 = np.concatenate([arr(L0_ffn_w2).transpose(0, 2, 1).reshape(-1, FEAT), arr(L0_ffn_sw2).T])
    w2 = np.concatenate([w2, np.zeros((TILES * P - w2.shape[0], FEAT), w2.dtype)]).reshape(TILES, P, FEAT)
    experts = np.concatenate([gate.reshape(TILES, P, FEAT), up.reshape(TILES, P, FEAT), w2], axis=2)

    arrays = {
        "x": x,
        "ctx_feat": c.transpose(0, 2, 1),
        "ctx_heads": ctx_heads,
        "experts": experts,
        "gate_w": arr(L0_ffn_gate_w).T.reshape(HALF, P, EXPERTS).transpose(1, 0, 2),
        "decay_bonus": np.stack([arr(L0_xattn_w), arr(L0_xattn_u)], 1).reshape(HALF, P, 2).transpose(1, 0, 2),
        "ffn_w": arr(L1_ffn_weight).reshape(HALF, P, FEAT).transpose(1, 0, 2),
        "ffn_scale": arr(L1_ffn_scale),
        "eye": np.eye(P, dtype=np.float32),
    }
    arrays = {name: np.ascontiguousarray(v) for name, v in arrays.items()}
    nc = bacc.Bacc("TRN2", target_bir_lowering=False, num_devices=1)
    args = [nc.dram_tensor(name, v.shape, mybir.dt.from_np(v.dtype), kind="ExternalInput").ap() for name, v in arrays.items()]
    out = nc.dram_tensor("out", (BATCH, POS, FEAT), F32, kind="ExternalOutput").ap()
    build(nc, *args, out)
    r = run_bass_kernel_spmd(nc, [arrays], core_ids=[0])
    return r.results[0]["out"]
```

```python
from contextlib import ExitStack

import concourse.bass as bass
from concourse import mybir

F32 = mybir.dt.float32
F32R = mybir.dt.float32r
F16 = mybir.dt.float16
ALU = mybir.AluOpType
ACT = mybir.ActivationFunctionType
AX_X = mybir.AxisListType.X

P = 128
BATCH, POS, FEAT = 16, 128, 256
HALF = FEAT // P
BB = 4
BLOCKS = BATCH // BB
TOK = BB * POS
EXPERTS, INNER, TOP_K = 16, 176, 6
SHARED = 2 * INNER
OPEN = -(-SHARED // P)
ROUTED = EXPERTS * INNER // P
TILES = OPEN + ROUTED
HEADS = 8
CH = POS // HEADS
PAIRS = HEADS // 2
STACK = 6 * CH
LN_EPS = 1e-5
BALL_EPS = 1e-7
MAX_NORM = 0.99
NEG = -1e38
CLAMP = 60.0

W_SCALE = 64.0
H_SCALE = 8.0
ROUTE_SCALE = H_SCALE * 0.5 / (W_SCALE * W_SCALE)

SLOTS = 3 * TILES
LAG = 2
WKV_START = -57
K_TURN, HALVES, HALF_GAP, Y_TURN = 5, 5, 16, 18
X2_NORM, X2_TURN, GATE, TOP, ROUTE = 42, 46, 50, 57, 61
ATTN_OFFSET = 8
ATTN_GAP, ATTN_LATE_GAP, ATTN_LAST_GAP = 13, 17, 10
FIRST_LAST = BATCH - BB
PLAN = dict(maxima=8, shift=17, exps=22, values=25, values_out=34, att_turn=35, x4_turn=39, ffn=41, v_split=14)
LAST_PLAN = dict(maxima=8, shift=17, exps=22, values=25, values_out=31, att_turn=36, x4_turn=39, ffn=41, v_split=17)
PLAN_END = 6
LOAD_LEAD, SPLIT_LEAD = 6, 6
MOE_FIRST = dict(pe=(0, 1, 2), dve=(), act=(0,), pool=())
FIRST_SLOT = WKV_START
LAST_SLOT = SLOTS * BLOCKS + ATTN_OFFSET + ATTN_LAST_GAP * (BB - 1) + LAST_PLAN["ffn"] + PLAN_END


def wkv_start(n):
    return WKV_START + SLOTS * n


def attn_plan(m):
    return LAST_PLAN if m >= FIRST_LAST else PLAN


def half_start(n, h):
    return HALVES + (HALF_GAP if n else 2) * h


def attn_start(m):
    gap = {BLOCKS - 1: ATTN_LAST_GAP, BLOCKS - 2: ATTN_LATE_GAP}.get(m // BB, ATTN_GAP)
    return SLOTS * (m // BB + 1) + ATTN_OFFSET + gap * (m % BB)


def qk_buffer(m):
    return m % 2 if m < BATCH - 2 else m % 4


def qk_uses(m):
    return sum(qk_buffer(b) == qk_buffer(m) for b in range(m + 1))


def qk_before(m):
    before = [b for b in range(m) if qk_buffer(b) == qk_buffer(m)]
    return before[-1] if before else None


def attn_steps(slot):
    return [(m, slot - attn_start(m)) for m in range(BATCH) if 0 <= slot - attn_start(m) <= attn_plan(m)["ffn"] + PLAN_END]


def wkv_steps(slot):
    return [(n, slot - wkv_start(n)) for n in range(BLOCKS) if 0 <= slot - wkv_start(n) < SLOTS]


def route_parts():
    parts, landed, had = [], [], [0, 0, 0]
    for r in range(ROUTED * BLOCKS):
        j = r % ROUTED
        cuts = []
        row = j * P
        while row < (j + 1) * P:
            e = row // INNER
            end = min((e + 1) * INNER, (j + 1) * P)
            cuts.append((e, row - j * P, end - j * P))
            row = end
        had[r % 3] += len(cuts)
        parts.append(cuts)
        landed.append(16 * had[r % 3])
    return parts, landed


def low_parts(k):
    first = 8 * FIRST_LAST
    late = max(0, k - first) // 2
    return k - late, late


def low_on_vector(k):
    return low_parts(k + 1)[1] > low_parts(k)[1]


def bank_uses():
    misc, score = {}, {}
    for slot in range(FIRST_SLOT, LAST_SLOT + 1):
        for m, a in attn_steps(slot):
            plan = attn_plan(m)
            if plan["maxima"] <= a < plan["maxima"] + 8:
                score[("max", m, a - plan["maxima"])] = len(score) + 1
            if a == plan["shift"]:
                misc[("shift", m)] = len(misc) + 1
            if plan["exps"] <= a < plan["exps"] + 8:
                score[("exp", m, a - plan["exps"])] = len(score) + 1
            if a == plan["att_turn"]:
                misc[("att", m)] = len(misc) + 1
            if a == plan["x4_turn"]:
                misc[("x4", m)] = len(misc) + 1
            if a == plan["ffn"]:
                misc[("ffn", m)] = len(misc) + 1
        for n, w in wkv_steps(slot):
            for h in range(HALF):
                if w == K_TURN + h:
                    misc[("k", n, h)] = len(misc) + 1
                if w == half_start(n, h) + Y_TURN:
                    misc[("y", n, h)] = len(misc) + 1
                if w == X2_TURN + 2 * h:
                    misc[("x2", n, h)] = len(misc) + 1
            if w == GATE:
                misc[("gate", n)] = len(misc) + 1
            if w == ROUTE:
                misc[("route", n)] = len(misc) + 1
    return misc, score


def score_banks(score):
    turn, had = {}, {}
    bank_of, before = {}, {}
    for key in sorted(score, key=score.get):
        spare = key[0] == "max" and key[1] // BB == BLOCKS - 1
        turn[spare] = turn.get(spare, -1) + 1
        bank_of[key] = turn[spare] % 2 + 2 * spare
        before[key] = had.get(bank_of[key])
        had[bank_of[key]] = key
    return bank_of, before


def build(nc, x, ctx_feat, ctx_heads, experts, gate_w, decay_bonus, ffn_w, ffn_scale, eye, out):
    misc_no, score_no = bank_uses()
    score_bank, score_before = score_banks(score_no)
    parts, parts_in = route_parts()
    c_scratch = nc.dram_tensor("c_scratch", (2, EXPERTS, TOK), F32, kind="Internal").ap()
    q_scratch = nc.dram_tensor("q_scratch", (4, 2, P, FEAT), F32, kind="Internal").ap()
    m_scratch = nc.dram_tensor("m_scratch", (4, HEADS, FEAT), F32, kind="Internal").ap()

    with ExitStack() as ctx:
        def sb(name, shape, dt=F32):
            return ctx.enter_context(nc.sbuf_tensor(name, shape, dt))

        def bank(name):
            return ctx.enter_context(nc.psum_tensor(name, [P, 512], F32))

        with ExitStack() as over:
            late_qz = [over.enter_context(nc.sbuf_tensor(f"late_qz{i}", [P, PAIRS, 2 * FEAT], F32R)) for i in range(2)]
            late_ks = [over.enter_context(nc.sbuf_tensor(f"late_ks{i}", [P, PAIRS, FEAT], F32R)) for i in range(2)]
        w13_hi = sb("w13_hi", [P, TILES, 2, HALF, P], F16)
        w13_lo = sb("w13_lo", [P, TILES, 2, HALF, P], F16)
        w2_hi = sb("w2_hi", [P, TILES, FEAT], F16)
        w2_lo = sb("w2_lo", [P, TILES, FEAT], F16)
        gw = sb("gw", [P, HALF, EXPERTS])
        gw_hi = sb("gw_hi", [P, HALF, EXPERTS], F16)
        gw_lo = sb("gw_lo", [P, HALF, EXPERTS], F16)
        arena = sb("arena", [P, 10 * FEAT])
        stage = [arena[:, 3 * FEAT * i:3 * FEAT * (i + 1)] for i in range(3)]
        ysb = arena[:, 0:HALF * TOK].rearrange("p (h t) -> p h t", h=HALF)
        kraw = arena[0:STACK, 4 * FEAT:8 * FEAT].rearrange("p (a k) -> p a k", a=PAIRS)
        vb = [arena[:, (8 + i) * FEAT:(9 + i) * FEAT].rearrange("p (h t) -> p h t", h=HALF) for i in range(2)]
        eye_sb = sb("eye_sb", [P, P])
        wu = sb("wu", [P, HALF, 2])
        ffn_sb = sb("ffn_sb", [P, HALF, FEAT])
        ffn_s = sb("ffn_s", [P, FEAT])
        neg_half = sb("neg_half", [P, BB])
        pos_half = sb("pos_half", [P, 1])
        res = [sb(f"res{i}", [P, BB, FEAT]) for i in range(BLOCKS)]
        xn = sb("xn", [P, BB, FEAT])
        vT = sb("vT", [P, HALF, BB, POS])
        kT = [sb(f"kT{h}", [P, BB, POS]) for h in range(HALF)]
        top = sb("top", [P, BB, POS + 1])
        num_s = sb("num_s", [P, BB, POS + 1])
        den_s = sb("den_s", [P, BB, POS + 1])
        keep = sb("keep", [P, BB, POS])
        take = sb("take", [P, BB, POS])
        now = sb("now", [P, BB, POS])
        take_v = sb("take_v", [P, BB, POS])
        now_v = sb("now_v", [P, BB, POS])
        stats = sb("stats", [P, BB, 6])
        mv = sb("mv", [P, BB, 2])
        ve = sb("ve", [P, BB])
        rstd = sb("rstd", [P, BB])
        lg = sb("lg", [P, BB, EXPERTS])
        lmax = sb("lmax", [P, BB])
        ex = sb("ex", [P, BB, EXPERTS])
        small = sb("small", [P, 4, BB])
        probs = sb("probs", [P, BB, EXPERTS + 2])
        top8 = sb("top8", [P, BB, 8])
        rest = sb("rest", [P, BB, EXPERTS + 2])
        route = sb("route", [P, BB, EXPERTS])
        cT = sb("cT", [EXPERTS, TOK])
        cb = [sb(f"cb{i}", [P, TOK]) for i in range(3)]
        xT_hi = [sb(f"xT_hi{i}", [P, HALF, TOK], F16) for i in range(2)]
        xT_lo = [sb(f"xT_lo{i}", [P, HALF, TOK], F16) for i in range(2)]
        th = sb("th", [P, TOK])
        hb = [sb(f"hb{i}", [P, TOK]) for i in range(2)]
        others = [t[:, :].rearrange("p (b t) -> p b t", b=BB) for t in (*cb, *hb)]
        def wkv_buffers(n, h):
            if (n, h) == (0, 1):
                return (*(r[:, :, 0:POS + 1] for r in res[:0:-1]), *others)
            return tuple(t[:, :, :] for t in (top, num_s, den_s, keep, take, now, take_v, now_v))
        h_hi = [sb(f"h_hi{i}", [P, TOK], F16) for i in range(LAG + 1)]
        h_lo = [sb(f"h_lo{i}", [P, TOK], F16) for i in range(LAG + 1)]
        stats3 = sb("stats3", [P, 6])
        mv3 = sb("mv3", [P, 2])
        ve3 = sb("ve3", [P, 1])
        rstd3 = sb("rstd3", [P, 1])
        q = sb("q", [P, FEAT])
        q_hi = sb("q_hi", [P, FEAT], F32R)
        q_lo = q[:, :].bitcast(F32R)
        qz = [sb(f"qz{i}", [P, PAIRS, 2 * FEAT], F32R) for i in range(2)] + late_qz
        ks = [sb(f"ks{i}", [P, PAIRS, FEAT], F32R) for i in range(2)] + late_ks
        v_hi = [sb(f"v_hi{i}", [P, HALF, HEADS, CH + 1], F16) for i in range(2)]
        v_lo = [sb(f"v_lo{i}", [P, HALF, HEADS, CH + 1], F16) for i in range(2)]
        mx = [sb(f"mx{i}", [P, HALF, HEADS]) for i in range(2)]
        shift = sb("shift", [HEADS, FEAT], F32R)
        pr = [sb(f"pr{i}", [P, 2 * FEAT]) for i in range(2)]
        pr_hi = [sb(f"pr_hi{i}", [P, 2 * FEAT], F16) for i in range(4)]
        pr_lo = [sb(f"pr_lo{i}", [P, 2 * FEAT], F16) for i in range(3)]
        rsum = sb("rsum", [P, HALF * HEADS])
        att = sb("att", [P, HALF, POS])
        stats4 = sb("stats4", [P, 6])
        mv4 = sb("mv4", [P, 2])
        ve4 = sb("ve4", [P, 1])
        rstd4 = sb("rstd4", [P, 1])
        x4n = sb("x4n", [P, FEAT])
        x4T = sb("x4T", [P, HALF, POS])
        fo = sb("fo", [P, FEAT])
        sc = sb("sc", [P, 12])

        gate_ps, up_ps = bank("gate_ps"), bank("up_ps")
        y_ps = [bank("y_ps0"), bank("y_ps1")]
        score_ps = [bank("score_ps0"), bank("score_ps1")]
        score_ps += [gate_ps, up_ps]
        av_ps, misc_ps = bank("av_ps"), bank("misc_ps")
        av = av_ps[:, 0:HALF * HEADS * (CH + 1)].rearrange("p (g c) -> p g c", c=CH + 1)

        def turn_bank(n, h):
            return up_ps if (n, h) == (0, 1) else misc_ps

        def sem(name):
            return ctx.enter_context(nc.semaphore(name))

        early_in = sem("early_in")
        consts_in = sem("consts_in")
        consts_set = sem("consts_set")
        gate_w_hi = sem("gate_w_hi")
        gate_w_lo = sem("gate_w_lo")
        x_in = sem("x_in")
        v_in = sem("v_in")
        var_ready = sem("var_ready")
        rstd_ready = sem("rstd_ready")
        xn_ready = sem("xn_ready")
        top_ready = sem("top_ready")
        own_ready = sem("own_ready")
        keep_ready = sem("keep_ready")
        take_ready = sem("take_ready")
        exps_ready = sem("exps_ready")
        take_v_ready = sem("take_v_ready")
        now_v_ready = sem("now_v_ready")
        yk_ready = sem("yk_ready")
        x2_hi_ready = sem("x2_hi_ready")
        dve_step = sem("dve_step")
        logits_exp = sem("logits_exp")
        w13_hi_ready = sem("w13_hi_ready")
        w13_lo_ready = sem("w13_lo_ready")
        w2_hi_ready = sem("w2_hi_ready")
        w2_lo_ready = sem("w2_lo_ready")
        gate_ready = sem("gate_ready")
        tanh_ready = sem("tanh_ready")
        gate_used = sem("gate_used")
        route_used = sem("route_used")
        route_set = sem("route_set")
        route_out = sem("route_out")
        route_in = [sem(f"route_in{i}") for i in range(3)]
        max_read = sem("max_read")
        exp_read = sem("exp_read")
        pr_hi_ready = sem("pr_hi_ready")
        pr_lo_ready = sem("pr_lo_ready")
        pr_lo_late = sem("pr_lo_late")
        v_hi_ready = sem("v_hi_ready")
        att_ready = sem("att_ready")
        up_ready = sem("up_ready")
        h_ready = sem("h_ready")
        h_hi_ready = sem("h_hi_ready")
        h_lo_ready = sem("h_lo_ready")
        y_done = sem("y_done")
        y_copied = sem("y_copied")
        y_turned = sem("y_turned")
        y_added = sem("y_added")
        var3_ready = sem("var3_ready")
        rstd3_ready = sem("rstd3_ready")
        q_ready = sem("q_ready")
        q_hi_ready = sem("q_hi_ready")
        q_lo_ready = sem("q_lo_ready")
        kraw_in = sem("kraw_in")
        ks_hi_ready = sem("ks_hi_ready")
        ks_ready = sem("ks_ready")
        vb_in = [sem(f"vb_in{i}") for i in range(2)]
        v_ready = sem("v_ready")
        q_out = [sem(f"q_out{i}") for i in range(4)]
        qz_in = [sem(f"qz_in{i}") for i in range(4)]
        spare_set = sem("spare_set")
        shift_out = sem("shift_out")
        shift_in = sem("shift_in")
        score_written = sem("score_written")
        av_done = sem("av_done")
        var4_ready = sem("var4_ready")
        rstd4_ready = sem("rstd4_ready")
        x4_ready = sem("x4_ready")
        misc_written = sem("misc_written")
        misc_read = sem("misc_read")
        square_ready = sem("square_ready")
        norm_ready = sem("norm_ready")
        norm1_ready = sem("norm1_ready")
        tanh1_ready = sem("tanh1_ready")
        res_ready = sem("res_ready")
        stored = sem("stored")
        stage_in = [sem(f"stage_in{i}") for i in range(3)]

        N_EARLY = 3
        N_CONSTS = 2
        N_SET = 17

        block = ctx.enter_context(nc.Block())

        @block.sync
        def _(sp):
            def load_const(dst, src):
                sp.dma_start(dst, src).then_inc(consts_in, 16)

            def load(n):
                sp.dma_start(res[n][:, :, :], x[BB * n:BB * n + BB].rearrange("b t c -> t b c")).then_inc(x_in, 16)
                if n == 0:
                    sp.dma_start(eye_sb[:, :], eye).then_inc(early_in, 16)
                    sp.dma_start(wu[:, :, :], decay_bonus).then_inc(early_in, 16)
                    sp.dma_start(gw[:, :, :], gate_w).then_inc(early_in, 16)
                if n >= 1:
                    sp.wait_ge(v_in, 32 * n)
                    sp.wait_ge(take_v_ready, 2 * n)
                    sp.wait_ge(now_v_ready, 2 * n)
                for h in range(HALF):
                    sp.dma_start(vT[:, h, :, :], ctx_feat[BB * n:BB * n + BB, h * P:(h + 1) * P, :].rearrange("b p t -> p b t")).then_inc(v_in, 16)
                if n == 0:
                    load_const(ffn_sb[:, :, :], ffn_w)
                    load_const(ffn_s[:, :], ffn_scale.partition_broadcast(P))

            def wkv(n, w):
                if w == 0:
                    load(n)
                if w == ROUTE + 1:
                    sp.wait_ge(misc_read, misc_no[("route", n)])
                    if n >= 1:
                        sp.wait_ge(route_out, 16 * n)
                    if n >= 2:
                        for i in range(3):
                            last = max(r for r in range(ROUTED * (n - 1)) if r % 3 == i)
                            sp.wait_ge(route_in[i], parts_in[last])
                    sp.dma_start(c_scratch[n % 2], cT[:, :]).then_inc(route_out, 16)

            def route(slot):
                t = (slot + 3) // 3
                n, j = t // TILES, t % TILES
                if slot % 3 == 0 and 0 <= t < TILES * BLOCKS and j >= OPEN:
                    r = ROUTED * n + j - OPEN
                    if j == OPEN:
                        sp.wait_ge(route_out, 16 * (n + 1))
                    if r >= 3:
                        sp.wait_ge(route_used, r - 2)
                        sp.wait_ge(route_in[r % 3], parts_in[r - 3])
                    for e, a, b in parts[r]:
                        sp.dma_start(cb[r % 3][a:b, :], c_scratch[n % 2, e].partition_broadcast(b - a)).then_inc(route_in[r % 3], 16)

            def weights(slot):
                if slot % 3 == 0 and 0 <= slot // 3 + LOAD_LEAD < TILES:
                    j = slot // 3 + LOAD_LEAD
                    if j >= 3:
                        sp.wait_ge(w13_hi_ready, j - 2)
                        sp.wait_ge(w13_lo_ready, j - 2)
                        sp.wait_ge(w2_lo_ready, j - 2)
                        sp.wait_ge(stage_in[j % 3], 16 * (j // 3))
                    sp.dma_start(stage[j % 3], experts[j]).then_inc(stage_in[j % 3], 16)

            def attention(m, a):
                plan = attn_plan(m)
                i = qk_buffer(m)
                if a == 0:
                    if m >= 1:
                        sp.wait_ge(ks_ready, m)
                        sp.wait_ge(kraw_in, 16 * m)
                        if m >= 2:
                            sp.wait_ge(v_ready, m - 1)
                            sp.wait_ge(vb_in[m % 2], 16 * (m // 2))
                    else:
                        sp.wait_ge(w2_lo_ready, TILES)
                        for s in range(3):
                            sp.wait_ge(stage_in[s], 16 * len(range(s, TILES, 3)))
                    sp.dma_start(kraw, ctx_heads[m]).then_inc(kraw_in, 16)
                    sp.dma_start(vb[m % 2], ctx_feat[m].rearrange("(h p) t -> p h t", p=P)).then_inc(vb_in[m % 2], 16)
                if a == 2:
                    sp.wait_ge(q_hi_ready, m + 1)
                    if qk_before(m) is not None:
                        sp.wait_ge(qz_in[i], 96 * (qk_uses(m) - 1))
                    sp.dma_start(q_scratch[i, 0], q_hi[:, :].bitcast(F32)).then_inc(q_out[i], 16)
                    sp.wait_ge(q_lo_ready, m + 1)
                    sp.dma_start(q_scratch[i, 1], q_lo.bitcast(F32)).then_inc(q_out[i], 16)
                if a == 4:
                    sp.wait_ge(q_out[i], 32 * qk_uses(m))
                    if qk_before(m) is not None:
                        sp.wait_ge(score_written, score_no[("exp", qk_before(m), 7)])
                    elif m >= 2:
                        sp.wait_ge(spare_set, 4)
                    for row, part, head, col in ((0, 0, 0, 0), (16, 1, 0, 0), (64, 0, 0, 0),
                                                 (32, 0, 4, FEAT), (48, 1, 4, FEAT), (80, 0, 4, FEAT)):
                        src = q_scratch[i, part, head * CH:(head + PAIRS) * CH, :].rearrange("(p c) t -> c p t", c=CH)
                        sp.dma_start(qz[i][row:row + CH, :, col:col + FEAT].bitcast(F32), src).then_inc(qz_in[i], 16)
                if a == plan["shift"] + 1:
                    sp.wait_ge(misc_read, misc_no[("shift", m)])
                    if qk_before(m) is not None:
                        sp.wait_ge(shift_in, 32 * (qk_before(m) + 1))
                    sp.dma_start(m_scratch[i], shift[:, :].bitcast(F32)).then_inc(shift_out, 16)
                    sp.wait_ge(shift_out, 16 * (m + 1))
                    for half in range(2):
                        sp.dma_start(qz[i][STACK + half:STACK + half + 1, :, half * FEAT:(half + 1) * FEAT].bitcast(F32),
                                     m_scratch[i:i + 1, half * PAIRS:(half + 1) * PAIRS, :]).then_inc(shift_in, 16)
                if a == plan["ffn"] + PLAN_END:
                    sp.wait_ge(res_ready, m + 1)
                    sp.dma_start(out[m], res[m // BB][:, m % BB, :]).then_inc(stored, 16)

            for slot in range(FIRST_SLOT, LAST_SLOT + 1):
                weights(slot)
                route(slot)
                for m, a in attn_steps(slot):
                    attention(m, a)
                for n, w in wkv_steps(slot):
                    wkv(n, w)
            sp.wait_ge(stored, 16 * BATCH)

        @block.gpsimd
        def _(pool):
            nc.gpsimd.memset(neg_half[:, :], -0.5).then_inc(consts_set, 1)
            nc.gpsimd.memset(pos_half[:, :], 0.5).then_inc(consts_set, 1)
            for h in range(HALF):
                for state, value in zip(wkv_buffers(0, h), (NEG, 0.0, 0.0)):
                    nc.gpsimd.memset(state[:, :, 0:1], value).then_inc(consts_set, 1)
            nc.gpsimd.memset(probs[:, :, EXPERTS:EXPERTS + 2], 3.0).then_inc(consts_set, 1)
            for i in range(2):
                nc.gpsimd.memset(v_hi[i][:, :, :, CH:CH + 1], 1.0).then_inc(consts_set, 1)
                nc.gpsimd.memset(v_lo[i][:, :, :, CH:CH + 1], 0.0).then_inc(consts_set, 1)
                nc.gpsimd.memset(qz[i][:, :, :].bitcast(F32), 0.0).then_inc(consts_set, 1)
            pool.wait_ge(consts_set, N_SET)
            def norm_scale(var_ready, no, dst, src, width, rstd_ready):
                pool.wait_ge(var_ready, no)
                nc.gpsimd.tensor_tensor(dst, src, neg_half[:, 0:width], ALU.pow).then_inc(rstd_ready, 1)

            def moe(slot):
                t, r = slot // 3, slot % 3
                if r == 2 and 0 <= t < TILES * BLOCKS:
                    pool.wait_ge(h_hi_ready, t + 1)
                    nc.gpsimd.tensor_tensor(h_lo[t % (LAG + 1)][:, :], hb[t % 2][:, :], h_hi[t % (LAG + 1)][:, :],
                                            ALU.subtract).then_inc(h_lo_ready, 1)

            def weights(slot):
                if slot % 3 == 0 and 0 <= slot // 3 + SPLIT_LEAD < TILES:
                    j = slot // 3 + SPLIT_LEAD
                    pool.wait_ge(w2_hi_ready, j + 1)
                    pool.wait_ge(w13_lo_ready, j + 1)
                    nc.gpsimd.tensor_tensor(w2_lo[:, j, :], stage[j % 3][:, 2 * FEAT:3 * FEAT], w2_hi[:, j, :],
                                            ALU.subtract).then_inc(w2_lo_ready, 1)

            def attention(m, a):
                plan = attn_plan(m)
                i = qk_buffer(m)
                if a == 0:
                    norm_scale(var3_ready, m + 1, rstd3[:, :], ve3[:, :], 1, rstd3_ready)
                if a == 1:
                    pool.wait_ge(q_hi_ready, m + 1)
                    nc.gpsimd.tensor_tensor(q_lo, q[:, :], q_hi[:, :].bitcast(F32), ALU.subtract).then_inc(q_lo_ready, 1)
                if a == plan["v_split"]:
                    pool.wait_ge(v_hi_ready, 2 * (m + 1))
                    for st in range(HALF):
                        ins = nc.gpsimd.tensor_tensor(v_lo[m % 2][:, st, :, 0:CH],
                                                      vb[m % 2][:, st, :].rearrange("p (h c) -> p h c", h=HEADS),
                                                      v_hi[m % 2][:, st, :, 0:CH], ALU.subtract)
                    ins.then_inc(v_ready, 1)
                if plan["exps"] + 1 <= a < plan["exps"] + 9 and not low_on_vector(8 * m + a - plan["exps"] - 1):
                    e = a - plan["exps"] - 1
                    pool.wait_ge(pr_hi_ready, 8 * m + e + 1)
                    if 8 * m + e >= 3:
                        pool.wait_ge(av_done, 8 * m + e - 2)
                    nc.gpsimd.tensor_tensor(pr_lo[(8 * m + e) % 3][:, :], pr[e % 2][:, :], pr_hi[e % 4][:, :],
                                            ALU.subtract).then_inc(pr_lo_ready, 1)
                if a == plan["att_turn"] + 1:
                    norm_scale(var4_ready, m + 1, rstd4[:, :], ve4[:, :], 1, rstd4_ready)
                if a == plan["ffn"] + 2:
                    pool.wait_ge(square_ready, m + 1)
                    nc.gpsimd.tensor_tensor(sc[:, 1:2], sc[:, 0:1], pos_half[:, :], ALU.pow).then_inc(norm_ready, 1)

            def wkv(n, w):
                if w == 0:
                    norm_scale(var_ready, 2 * n + 1, rstd[:, :], ve[:, :], BB, rstd_ready)
                if w == X2_NORM:
                    norm_scale(var_ready, 2 * n + 2, rstd[:, :], ve[:, :], BB, rstd_ready)
                for h in range(HALF):
                    c = 2 * n + h
                    top, _, _, keep, take, now, take_v, now_v = wkv_buffers(n, h)
                    if w == half_start(n, h) + 1:
                        pool.wait_ge(top_ready, c + 1)
                        nc.gpsimd.tensor_tensor(keep, top[:, :, 0:POS], top[:, :, 1:POS + 1], ALU.subtract).then_inc(keep_ready, 1)
                        if n >= 1:
                            nc.gpsimd.tensor_tensor(take, kT[h][:, :, :], top[:, :, 1:POS + 1],
                                                    ALU.subtract).then_inc(take_ready, 1)
                    if w == half_start(n, h) + 3:
                        if c == 0:
                            pool.wait_ge(v_in, 32)
                        elif h == 0:
                            pool.wait_ge(v_in, 32 * (n + 1))
                        pool.wait_ge(exps_ready, 3 * c + 3)
                        if n >= 1:
                            pool.wait_ge(misc_written, misc_no[("y", (c - 1) // 2, (c - 1) % 2)])
                            nc.gpsimd.tensor_tensor(take_v, take, vT[:, h, :, :], ALU.mult).then_inc(take_v_ready, 1)
                        nc.gpsimd.tensor_tensor(now_v, now, vT[:, h, :, :], ALU.mult).then_inc(now_v_ready, 1)

            for slot in range(FIRST_SLOT, LAST_SLOT + 1):
                moe_first = slot % 3 in MOE_FIRST["pool"]
                if moe_first:
                    moe(slot)
                for m, a in attn_steps(slot):
                    attention(m, a)
                for n, w in wkv_steps(slot):
                    wkv(n, w)
                if not moe_first:
                    moe(slot)
                weights(slot)

        @block.scalar
        def _(act):
            def moe(slot):
                t, r = slot // 3, slot % 3
                if 0 <= t < TILES * BLOCKS:
                    if r == 0:
                        act.wait_ge(gate_ready, t + 1)
                        if t >= 1:
                            act.wait_ge(h_ready, t)
                        nc.scalar.activation(th[:, :], gate_ps[:, :], ACT.Tanh, scale=0.5 / W_SCALE).then_inc(tanh_ready, 1)
                    if r == 2:
                        act.wait_ge(h_ready, t + 1)
                        if t > LAG:
                            act.wait_ge(y_done, t - LAG)
                        nc.scalar.activation(h_hi[t % (LAG + 1)][:, :], hb[t % 2][:, :], ACT.Copy).then_inc(h_hi_ready, 1)
                n = slot // SLOTS - 1
                if 0 <= n < BLOCKS and slot % SLOTS == 3 * LAG - 1:
                    act.wait_ge(y_done, TILES * (n + 1))
                    if n >= 1:
                        act.wait_ge(y_turned, n)
                    for c in range(HALF):
                        nc.scalar.activation(ysb[:, c, :], y_ps[c][:, :], ACT.Copy,
                                             scale=1.0 / (H_SCALE * W_SCALE)).then_inc(y_copied, 1)

            def weights(slot):
                if slot % 3 == 0 and 0 <= slot // 3 + SPLIT_LEAD < TILES:
                    j = slot // 3 + SPLIT_LEAD
                    act.wait_ge(stage_in[j % 3], 16 * (j // 3 + 1))
                    nc.scalar.activation(w13_hi[:, j, :, :, :].rearrange("p a b c -> p (a b c)"),
                                         stage[j % 3][:, 0:2 * FEAT], ACT.Copy, scale=W_SCALE).then_inc(w13_hi_ready, 1)
                    act.wait_ge(w13_lo_ready, j + 1)
                    nc.scalar.activation(w2_hi[:, j, :], stage[j % 3][:, 2 * FEAT:3 * FEAT], ACT.Copy).then_inc(w2_hi_ready, 1)

            def attention(m, a):
                plan = attn_plan(m)
                i = qk_buffer(m)
                if a == 1:
                    act.wait_ge(q_ready, m + 1)
                    if m >= 1:
                        act.wait_ge(q_out[qk_buffer(m - 1)], 32 * qk_uses(m - 1))
                    nc.scalar.activation(q_hi[:, :], q[:, :], ACT.Copy).then_inc(q_hi_ready, 1)
                if a == 2:
                    act.wait_ge(kraw_in, 16 * (m + 1))
                    if qk_before(m) is not None:
                        act.wait_ge(score_written, score_no[("exp", qk_before(m), 7)])
                    elif m >= 2:
                        act.wait_ge(spare_set, 4)
                    nc.scalar.activation(ks[i][0:STACK, :, :], kraw, ACT.Copy).then_inc(ks_hi_ready, 1)
                if a == plan["shift"]:
                    act.wait_ge(misc_written, misc_no[("shift", m)])
                    if m >= 1:
                        act.wait_ge(shift_out, 16 * m)
                    nc.scalar.activation(shift[:, :], misc_ps[0:HEADS, 0:FEAT], ACT.Copy, scale=-1.0).then_inc(misc_read, 1)
                if plan["exps"] <= a < plan["exps"] + 8:
                    e = a - plan["exps"]
                    no = score_no[("exp", m, e)]
                    act.wait_ge(score_written, no)
                    if 8 * m + e >= 2:
                        act.wait_ge(pr_lo_ready, low_parts(8 * m + e - 1)[0])
                        if low_parts(8 * m + e - 1)[1]:
                            act.wait_ge(pr_lo_late, low_parts(8 * m + e - 1)[1])
                    nc.scalar.activation(pr[e % 2][:, :], score_ps[score_bank[("exp", m, e)]][:, :], ACT.Exp,
                                         scale=1.0 / CH).then_inc(exp_read, 1)
                    act.wait_ge(exp_read, 8 * m + e + 1)
                    if 8 * m + e >= 4:
                        act.wait_ge(av_done, 8 * m + e - 3)
                    nc.scalar.activation(pr_hi[e % 4][:, :], pr[e % 2][:, :], ACT.Copy).then_inc(pr_hi_ready, 1)
                if a == plan["v_split"]:
                    act.wait_ge(vb_in[m % 2], 16 * (m // 2 + 1))
                    if m >= 2:
                        act.wait_ge(av_done, 8 * (m - 1))
                    for st in range(HALF):
                        nc.scalar.activation(v_hi[m % 2][:, st, :, 0:CH], vb[m % 2][:, st, :].rearrange("p (h c) -> p h c", h=HEADS),
                                             ACT.Copy).then_inc(v_hi_ready, 1)
                if a == plan["x4_turn"]:
                    act.wait_ge(misc_written, misc_no[("x4", m)])
                    nc.scalar.activation(x4T[:, :, :], misc_ps[:, 0:FEAT].rearrange("p (h t) -> p h t", h=HALF),
                                         ACT.Copy).then_inc(misc_read, 1)
                if a == plan["ffn"] + 3:
                    act.wait_ge(norm1_ready, m + 1)
                    nc.scalar.activation(sc[:, 3:4], sc[:, 2:3], ACT.Tanh).then_inc(tanh1_ready, 1)

            def wkv(n, w):
                for h in range(HALF):
                    c = 2 * n + h
                    if w == K_TURN + h:
                        act.wait_ge(misc_written, misc_no[("k", n, h)])
                        nc.scalar.activation(kT[h][:, :, :], turn_bank(n, h)[:, :].rearrange("p (b t) -> p b t", b=BB),
                                             ACT.Copy).then_inc(misc_read, 1)
                    if w == half_start(n, h) + 2:
                        if c == 0:
                            act.wait_ge(early_in, 16 * N_EARLY)
                        _, _, _, keep, take, now, _, _ = wkv_buffers(n, h)
                        act.wait_ge(keep_ready, c + 1)
                        nc.scalar.activation(keep, keep, ACT.Exp, bias=wu[:, h, 0:1]).then_inc(exps_ready, 1)
                        act.wait_ge(take_ready, c + 1)
                        nc.scalar.activation(take, take, ACT.Exp).then_inc(exps_ready, 1)
                        act.wait_ge(own_ready, c + 1)
                        nc.scalar.activation(now, now, ACT.Exp).then_inc(exps_ready, 1)
                    if w == X2_TURN + 2 * h:
                        if n >= 2:
                            act.wait_ge(up_ready, TILES * (n - 1))
                        act.wait_ge(misc_written, misc_no[("x2", n, h)])
                        nc.scalar.activation(xT_hi[n % 2][:, h, :], turn_bank(n, h)[:, :], ACT.Copy).then_inc(x2_hi_ready, 1)
                if w == GATE:
                    act.wait_ge(misc_read, misc_no[("gate", n)])
                    nc.scalar.activation(ex[:, :, :], lg[:, :, :], ACT.Exp, scale=1.0 / W_SCALE).then_inc(logits_exp, 1)
                if w == ROUTE:
                    act.wait_ge(misc_written, misc_no[("route", n)])
                    if n >= 1:
                        act.wait_ge(route_out, 16 * n)
                    nc.scalar.activation(cT[:, :], misc_ps[0:EXPERTS, :], ACT.Copy).then_inc(misc_read, 1)

            act.wait_ge(early_in, 16 * N_EARLY)
            nc.scalar.activation(gw_hi[:, :, :], gw[:, :, :], ACT.Copy, scale=W_SCALE).then_inc(gate_w_hi, 1)
            for slot in range(FIRST_SLOT, LAST_SLOT + 1):
                moe_first = slot % 3 in MOE_FIRST["act"]
                if moe_first:
                    moe(slot)
                for m, a in attn_steps(slot):
                    attention(m, a)
                for n, w in wkv_steps(slot):
                    wkv(n, w)
                if not moe_first:
                    moe(slot)
                weights(slot)

        @block.vector
        def _(dve):
            steps = [0]

            def link(ins):
                steps[0] += 1
                ins.then_inc(dve_step, 1)
                dve.wait_ge(dve_step, steps[0])

            def norm_stats(xs, st, mean_var, var_eps, var_ready):
                for b, xb in enumerate(xs):
                    ins = nc.vector.bn_stats(st[b], xb)
                link(ins)
                for b in range(len(xs)):
                    ins = nc.vector.bn_aggr(mean_var[b], st[b])
                link(ins)
                nc.vector.tensor_scalar(var_eps[0], var_eps[1], LN_EPS, None, ALU.add).then_inc(var_ready, 1)

            def moe(slot):
                t, r = slot // 3, slot % 3
                if 0 <= t < TILES * BLOCKS:
                    if r == 0:
                        dve.wait_ge(tanh_ready, t + 1)
                        nc.vector.scalar_tensor_tensor(th[:, :], th[:, :], 1.0, gate_ps[:, :], ALU.add,
                                                       ALU.mult).then_inc(gate_used, 1)
                    if r == 1:
                        j = t % TILES
                        dve.wait_ge(gate_used, t + 1)
                        if j >= OPEN:
                            c = ROUTED * (t // TILES) + j - OPEN
                            dve.wait_ge(route_in[c % 3], parts_in[c])
                            nc.vector.tensor_tensor(th[:, :], th[:, :], cb[c % 3][:, :], ALU.mult).then_inc(route_used, 1)
                            dve.wait_ge(route_used, c + 1)
                        dve.wait_ge(up_ready, t + 1)
                        if t >= 2:
                            dve.wait_ge(h_lo_ready, t - 1)
                        if j >= OPEN:
                            nc.vector.tensor_tensor(hb[t % 2][:, :], th[:, :], up_ps[:, :], ALU.mult).then_inc(h_ready, 1)
                        else:
                            nc.vector.scalar_tensor_tensor(hb[t % 2][:, :], th[:, :], ROUTE_SCALE, up_ps[:, :], ALU.mult,
                                                           ALU.mult).then_inc(h_ready, 1)
                if slot == SLOTS * BLOCKS:
                    dve.wait_ge(up_ready, TILES * BLOCKS)
                    for i in (2, 3):
                        nc.vector.memset(qz[i][:, :, :].bitcast(F32), 0.0).then_inc(spare_set, 1)
                        nc.vector.memset(ks[i][STACK:P, :, :].bitcast(F32), 1.0).then_inc(spare_set, 1)
                n = slot // SLOTS - 1
                if 0 <= n < BLOCKS and slot % SLOTS == 3 * LAG + 1:
                    dve.wait_ge(y_turned, n + 1)
                    for c in range(2):
                        part = res[n][:, 2 * c:2 * c + 2, :]
                        ins = nc.vector.tensor_tensor(part, part, y_ps[c][:, :].rearrange("p (b f) -> p b f", b=2), ALU.add)
                    ins.then_inc(y_added, 1)
                    dve.wait_ge(y_added, n + 1)

            def weights(slot):
                if slot % 3 == 0 and 0 <= slot // 3 + SPLIT_LEAD < TILES:
                    j = slot // 3 + SPLIT_LEAD
                    dve.wait_ge(stage_in[j % 3], 16 * (j // 3 + 1))
                    part = stage[j % 3][:, 2 * FEAT:3 * FEAT]
                    nc.vector.tensor_scalar(part, part, W_SCALE, None, ALU.mult)
                    dve.wait_ge(w13_hi_ready, j + 1)
                    nc.vector.scalar_tensor_tensor(w13_lo[:, j, :, :, :].rearrange("p a b c -> p (a b c)"),
                                                   stage[j % 3][:, 0:2 * FEAT], W_SCALE,
                                                   w13_hi[:, j, :, :, :].rearrange("p a b c -> p (a b c)"),
                                                   ALU.mult, ALU.subtract).then_inc(w13_lo_ready, 1)

            def attention(m, a):
                plan = attn_plan(m)
                xb = res[m // BB][:, m % BB, :]
                if a == 0:
                    norm_stats([xb], [stats3[:, :]], [mv3[:, :]], (ve3[:, :], mv3[:, 1:2]), var3_ready)
                if a == 1:
                    dve.wait_ge(rstd3_ready, m + 1)
                    if m >= 1:
                        dve.wait_ge(q_out[qk_buffer(m - 1)], 32 * qk_uses(m - 1))
                    nc.vector.tensor_scalar(q[:, :], xb, mv3[:, 0:1], rstd3[:, 0:1], ALU.subtract, ALU.mult).then_inc(q_ready, 1)
                if a == 3:
                    dve.wait_ge(ks_hi_ready, m + 1)
                    low = ks[qk_buffer(m)][64:STACK, :, :]
                    nc.vector.tensor_tensor(low, kraw[64:STACK, :, :], low.bitcast(F32), ALU.subtract).then_inc(ks_ready, 1)
                if plan["maxima"] <= a < plan["maxima"] + 8:
                    v = a - plan["maxima"]
                    p, tt = v // 2, v % 2
                    no = score_no[("max", m, v)]
                    dve.wait_ge(score_written, no)
                    dst = mx[m % 2][:, tt, :].rearrange("q (a p) -> q a p", a=2)[:, :, p]
                    nc.vector.tensor_reduce(dst, score_ps[score_bank[("max", m, v)]][:, :].rearrange("q (a k) -> q a k", a=2), AX_X,
                                            ALU.max).then_inc(max_read, 1)
                if plan["exps"] + 1 <= a < plan["exps"] + 9 and low_on_vector(8 * m + a - plan["exps"] - 1):
                    e = a - plan["exps"] - 1
                    dve.wait_ge(pr_hi_ready, 8 * m + e + 1)
                    dve.wait_ge(av_done, 8 * m + e - 2)
                    nc.vector.tensor_tensor(pr_lo[(8 * m + e) % 3][:, :], pr[e % 2][:, :], pr_hi[e % 4][:, :],
                                            ALU.subtract).then_inc(pr_lo_late, 1)
                if a == plan["values_out"]:
                    dve.wait_ge(av_done, 8 * (m + 1))
                    link(nc.vector.reciprocal(rsum[:, :], av[:, :, CH]))
                    if m >= 1:
                        dve.wait_ge(misc_written, misc_no[("att", m - 1)])
                    nc.vector.tensor_tensor(att[:, :, :].rearrange("p t (h c) -> p (t h) c", h=HEADS), av[:, :, 0:CH],
                                            rsum[:, :].unsqueeze(2).to_broadcast([P, HALF * HEADS, CH]), ALU.mult).then_inc(att_ready, 1)
                if a == plan["att_turn"]:
                    dve.wait_ge(misc_written, misc_no[("att", m)])
                    nc.vector.tensor_tensor(xb, xb, misc_ps[:, 0:FEAT], ALU.add).then_inc(misc_read, 1)
                    dve.wait_ge(misc_read, misc_no[("att", m)])
                if a == plan["att_turn"] + 1:
                    norm_stats([xb], [stats4[:, :]], [mv4[:, :]], (ve4[:, :], mv4[:, 1:2]), var4_ready)
                if a == plan["att_turn"] + 2:
                    dve.wait_ge(rstd4_ready, m + 1)
                    nc.vector.tensor_scalar(x4n[:, :], xb, mv4[:, 0:1], rstd4[:, 0:1], ALU.subtract, ALU.mult).then_inc(x4_ready, 1)
                if a == plan["ffn"]:
                    dve.wait_ge(misc_written, misc_no[("ffn", m)])
                    if m == 0:
                        dve.wait_ge(consts_in, 16 * N_CONSTS)
                    nc.vector.tensor_tensor(fo[:, :], misc_ps[:, 0:FEAT], ffn_s[:, :], ALU.mult).then_inc(misc_read, 1)
                    dve.wait_ge(misc_read, misc_no[("ffn", m)])
                    nc.vector.tensor_tensor_reduce(x4n[:, :], fo[:, :], fo[:, :], 1.0, 0.0, ALU.mult, ALU.add,
                                                   sc[:, 0:1]).then_inc(square_ready, 1)
                if a == plan["ffn"] + 2:
                    dve.wait_ge(norm_ready, m + 1)
                    nc.vector.tensor_scalar(sc[:, 2:3], sc[:, 1:2], BALL_EPS, None, ALU.max).then_inc(norm1_ready, 1)
                    dve.wait_ge(norm1_ready, m + 1)
                    link(nc.vector.tensor_scalar(sc[:, 4:5], sc[:, 2:3], BALL_EPS, None, ALU.add))
                    link(nc.vector.reciprocal(sc[:, 5:6], sc[:, 4:5]))
                if a == plan["ffn"] + 4:
                    dve.wait_ge(tanh1_ready, m + 1)
                    link(nc.vector.tensor_tensor(sc[:, 6:7], sc[:, 3:4], sc[:, 5:6], ALU.mult))
                    link(nc.vector.tensor_tensor(sc[:, 7:8], sc[:, 1:2], sc[:, 6:7], ALU.mult))
                    link(nc.vector.tensor_scalar(sc[:, 8:9], sc[:, 7:8], BALL_EPS, None, ALU.max))
                    link(nc.vector.reciprocal(sc[:, 9:10], sc[:, 8:9]))
                    link(nc.vector.tensor_scalar(sc[:, 10:11], sc[:, 9:10], MAX_NORM, 1.0, ALU.mult, ALU.min))
                    link(nc.vector.tensor_tensor(sc[:, 11:12], sc[:, 10:11], sc[:, 6:7], ALU.mult))
                    nc.vector.scalar_tensor_tensor(xb, fo[:, :], sc[:, 11:12], xb, ALU.mult, ALU.add).then_inc(res_ready, 1)

            def block_norm(n):
                r = res[n]
                norm_stats([r[:, b, :] for b in range(BB)], [stats[:, b, :] for b in range(BB)],
                           [mv[:, b, :] for b in range(BB)], (ve[:, :], mv[:, :, 1]), var_ready)

            def block_normed(n, k):
                dve.wait_ge(rstd_ready, 2 * n + k + 1)
                for b in range(BB):
                    ins = nc.vector.tensor_scalar(xn[:, b, :], res[n][:, b, :], mv[:, b, 0:1], rstd[:, b:b + 1],
                                                  ALU.subtract, ALU.mult)
                ins.then_inc(xn_ready, 1)

            def wkv(n, w):
                if w == 0:
                    dve.wait_ge(x_in, 16 * (n + 1))
                    block_norm(n)
                if w == 1:
                    if n >= 1:
                        dve.wait_ge(misc_written, misc_no[("x2", n - 1, 1)])
                    block_normed(n, 0)
                for h in range(HALF):
                    c = 2 * n + h
                    u = w - half_start(n, h)
                    top, num, den, keep, take, now, take_v, now_v = wkv_buffers(n, h)
                    y = take_v
                    if u == 0:
                        if c == 0:
                            dve.wait_ge(early_in, 16 * N_EARLY)
                            dve.wait_ge(consts_set, N_SET)
                        dve.wait_ge(misc_read, misc_no[("k", n, h)])
                        for b in range(BB):
                            ins = nc.vector.tensor_tensor_scan(top[:, b, 1:POS + 1], wu[:, h, 0:1].to_broadcast([P, POS]),
                                                               kT[h][:, b, :], NEG, ALU.add, ALU.max)
                        ins.then_inc(top_ready, 1)
                        dve.wait_ge(top_ready, c + 1)
                    if u == 1:
                        if n == 0:
                            nc.vector.tensor_tensor(take, kT[h][:, :, :], top[:, :, 1:POS + 1], ALU.subtract).then_inc(take_ready, 1)
                        link(nc.vector.scalar_tensor_tensor(now, kT[h][:, :, :], wu[:, h, 1:2], top[:, :, 0:POS],
                                                            ALU.add, ALU.subtract))
                        nc.vector.tensor_scalar(now, now, CLAMP, None, ALU.min).then_inc(own_ready, 1)
                    if u == 3:
                        dve.wait_ge(exps_ready, 3 * c + 3)
                        for b in range(BB):
                            nc.vector.tensor_tensor_scan(den[:, b, 1:POS + 1], keep[:, b, :], take[:, b, :], 0.0,
                                                         ALU.mult, ALU.add)
                        if n == 0:
                            dve.wait_ge(v_in, 32)
                            nc.vector.tensor_tensor(take_v, take, vT[:, h, :, :], ALU.mult).then_inc(take_v_ready, 1)
                    if u == 5:
                        dve.wait_ge(take_v_ready, c + 1)
                        for b in range(BB):
                            ins = nc.vector.tensor_tensor_scan(num[:, b, 1:POS + 1], keep[:, b, :], take_v[:, b, :], 0.0,
                                                               ALU.mult, ALU.add)
                        link(ins)
                    if u == 6:
                        dve.wait_ge(now_v_ready, c + 1)
                        nc.vector.tensor_tensor(y, num[:, :, 0:POS], now_v, ALU.add)
                        link(nc.vector.tensor_tensor(now, den[:, :, 0:POS], now, ALU.add))
                    if u in (8, 9):
                        lo = 2 * (u - 8)
                        link(nc.vector.reciprocal(now[:, lo:lo + 2, :], now[:, lo:lo + 2, :]))
                    if u == 11:
                        nc.vector.tensor_tensor(y, y, now, ALU.mult).then_inc(yk_ready, 1)
                    if u == Y_TURN:
                        dve.wait_ge(misc_written, misc_no[("y", n, h)])
                        part = res[n][:, :, h * P:(h + 1) * P]
                        nc.vector.tensor_tensor(part, part, misc_ps[:, :].rearrange("p (b f) -> p b f", b=BB),
                                                ALU.add).then_inc(misc_read, 1)
                if w == X2_NORM:
                    dve.wait_ge(misc_read, misc_no[("y", n, 1)])
                    block_norm(n)
                if w == X2_NORM + 1:
                    block_normed(n, 1)
                for h in range(HALF):
                    if w == X2_TURN + 2 * h:
                        dve.wait_ge(x2_hi_ready, 2 * n + h + 1)
                        nc.vector.tensor_tensor(xT_lo[n % 2][:, h, :], turn_bank(n, h)[:, :], xT_hi[n % 2][:, h, :],
                                                ALU.subtract).then_inc(misc_read, 1)
                if w == GATE:
                    dve.wait_ge(misc_written, misc_no[("gate", n)])
                    logits = misc_ps[:, 0:BB * EXPERTS].rearrange("p (b e) -> p b e", b=BB)
                    link(nc.vector.tensor_reduce(lmax[:, :], logits, AX_X, ALU.max))
                    nc.vector.tensor_tensor(lg[:, :, :], logits, lmax[:, :].unsqueeze(2).to_broadcast([P, BB, EXPERTS]),
                                            ALU.subtract).then_inc(misc_read, 1)
                if w == TOP:
                    dve.wait_ge(logits_exp, n + 1)
                    link(nc.vector.tensor_reduce(small[:, 0, :], ex[:, :, :], AX_X, ALU.add))
                    link(nc.vector.reciprocal(small[:, 1, :], small[:, 0, :]))
                    link(nc.vector.tensor_tensor(probs[:, :, 0:EXPERTS], ex[:, :, :],
                                                 small[:, 1, :].unsqueeze(2).to_broadcast([P, BB, EXPERTS]), ALU.mult))
                if w == TOP + 1:
                    for b in range(BB):
                        ins = nc.vector.max(top8[:, b, :], probs[:, b, :])
                    link(ins)
                    for b in range(BB):
                        ins = nc.vector.match_replace(rest[:, b, :], top8[:, b, :], probs[:, b, :], 0.0)
                    link(ins)
                if w == TOP + 2:
                    if n >= 1:
                        dve.wait_ge(misc_written, misc_no[("route", n - 1)])
                    link(nc.vector.tensor_tensor(route[:, :, :], probs[:, :, 0:EXPERTS], rest[:, :, 0:EXPERTS], ALU.subtract))
                    link(nc.vector.tensor_reduce(small[:, 2, :], route[:, :, :], AX_X, ALU.add))
                    link(nc.vector.tensor_scalar(small[:, 2, :], small[:, 2, :], 1e-20, None, ALU.add))
                    link(nc.vector.reciprocal(small[:, 3, :], small[:, 2, :]))
                    link(nc.vector.tensor_scalar(small[:, 3, :], small[:, 3, :], ROUTE_SCALE, None, ALU.mult))
                    nc.vector.tensor_tensor(route[:, :, :], route[:, :, :],
                                            small[:, 3, :].unsqueeze(2).to_broadcast([P, BB, EXPERTS]), ALU.mult).then_inc(route_set, 1)

            for i in range(2):
                nc.vector.memset(ks[i][STACK:P, :, :].bitcast(F32), 1.0).then_inc(consts_set, 1)
            dve.wait_ge(gate_w_hi, 1)
            nc.vector.scalar_tensor_tensor(gw_lo[:, :, :], gw[:, :, :], W_SCALE, gw_hi[:, :, :], ALU.mult,
                                           ALU.subtract).then_inc(gate_w_lo, 1)
            for slot in range(FIRST_SLOT, LAST_SLOT + 1):
                moe_first = slot % 3 in MOE_FIRST["dve"]
                if moe_first:
                    moe(slot)
                for m, a in attn_steps(slot):
                    attention(m, a)
                for n, w in wkv_steps(slot):
                    wkv(n, w)
                if not moe_first:
                    moe(slot)
                weights(slot)

        @block.tensor
        def _(pe):
            def misc_free(key):
                if misc_no[key] > 1:
                    pe.wait_ge(misc_read, misc_no[key] - 1)

            def score_free(key):
                if score_before[key] is not None:
                    kind, m, u = score_before[key]
                    pe.wait_ge(max_read if kind == "max" else exp_read, 8 * m + u + 1)
                elif score_bank[key] >= 2:
                    pe.wait_ge(h_ready, TILES * BLOCKS)

            def rows(bank_ap, n, j, gu):
                i = n % 2
                for k in range(HALF):
                    for wt, xt in ((w13_hi, xT_hi), (w13_lo, xT_hi), (w13_hi, xT_lo)):
                        last = k == HALF - 1 and xt is xT_lo
                        ins = nc.tensor.matmul(bank_ap, wt[:, j, gu, k, :], xt[i][:, k, :],
                                               start=(k == 0 and wt is w13_hi and xt is xT_hi), stop=last)
                return ins

            def down(t):
                n, j = t // TILES, t % TILES
                pe.wait_ge(h_lo_ready, t + 1)
                if n == 0:
                    pe.wait_ge(w2_lo_ready, j + 1)
                elif j == 0:
                    pe.wait_ge(y_added, n)
                for c in range(HALF):
                    cols = slice(c * P, (c + 1) * P)
                    nc.tensor.matmul(y_ps[c][:, :], w2_hi[:, j, cols], h_hi[t % (LAG + 1)][:, :], start=(j == 0), stop=False)
                    nc.tensor.matmul(y_ps[c][:, :], w2_lo[:, j, cols], h_hi[t % (LAG + 1)][:, :], start=False, stop=False)
                    ins = nc.tensor.matmul(y_ps[c][:, :], w2_hi[:, j, cols], h_lo[t % (LAG + 1)][:, :], start=False,
                                           stop=(j == TILES - 1))
                ins.then_inc(y_done, 1)

            def moe(slot):
                t, r = slot // 3, slot % 3
                n, j = t // TILES, t % TILES
                if 0 <= t < TILES * BLOCKS:
                    if r == 0:
                        if j == 0:
                            pe.wait_ge(misc_read, misc_no[("x2", n, 1)])
                        if n == 0:
                            pe.wait_ge(w13_lo_ready, j + 1)
                        if t >= 1:
                            pe.wait_ge(gate_used, t)
                        rows(gate_ps[:, :], n, j, 0).then_inc(gate_ready, 1)
                    if r == 1:
                        if t >= 1:
                            pe.wait_ge(h_ready, t)
                        rows(up_ps[:, :], n, j, 1).then_inc(up_ready, 1)
                if r == 2 and 0 <= t - LAG < TILES * BLOCKS:
                    down(t - LAG)
                b = slot // SLOTS - 1
                if 0 <= b < BLOCKS and slot % SLOTS == 3 * LAG + 1:
                    pe.wait_ge(y_copied, 2 * (b + 1))
                    for bb in range(BB):
                        for c in range(HALF):
                            col = (bb % 2) * FEAT + c * P
                            ins = nc.tensor.transpose(y_ps[bb // 2][:, col:col + P], ysb[:, c, bb * P:(bb + 1) * P], eye_sb[:, :])
                    ins.then_inc(y_turned, 1)

            def attention(m, a):
                plan = attn_plan(m)
                i = qk_buffer(m)
                if plan["maxima"] <= a < plan["maxima"] + 8:
                    v = a - plan["maxima"]
                    p, tt = v // 2, v % 2
                    if v == 0:
                        if m == 0:
                            pe.wait_ge(consts_set, N_SET)
                            pe.wait_ge(consts_in, 16 * N_CONSTS)
                        pe.wait_ge(qz_in[i], 96 * qk_uses(m))
                        pe.wait_ge(ks_ready, m + 1)
                    score_free(("max", m, v))
                    for half in range(2):
                        col = half * FEAT + tt * P
                        ins = nc.tensor.matmul(score_ps[score_bank[("max", m, v)]][:, half * FEAT:(half + 1) * FEAT], qz[i][0:STACK, p, col:col + P],
                                               ks[i][0:STACK, p, :], start=True, stop=True)
                    ins.then_inc(score_written, 1)
                if a == plan["shift"]:
                    misc_free(("shift", m))
                    pe.wait_ge(max_read, 8 * (m + 1))
                    for tt in range(HALF):
                        ins = nc.tensor.transpose(misc_ps[0:HEADS, tt * P:(tt + 1) * P], mx[m % 2][:, tt, :], eye_sb[:, :])
                    ins.then_inc(misc_written, 1)
                if plan["exps"] <= a < plan["exps"] + 8:
                    e = a - plan["exps"]
                    p, st = e // 2, e % 2
                    if e == 0:
                        pe.wait_ge(shift_in, 32 * (m + 1))
                    score_free(("exp", m, e))
                    nc.tensor.matmul(score_ps[score_bank[("exp", m, e)]][:, :], ks[i][0:STACK + 2, p, st * P:(st + 1) * P], qz[i][0:STACK + 2, p, :],
                                     start=True, stop=True).then_inc(score_written, 1)
                if plan["values"] <= a < plan["values"] + 8:
                    e = a - plan["values"]
                    p, st = e // 2, e % 2
                    if e == 0:
                        pe.wait_ge(v_ready, m + 1)
                        if m >= 1:
                            pe.wait_ge(att_ready, m)
                    pe.wait_ge(pr_lo_ready, low_parts(8 * m + e + 1)[0])
                    if low_parts(8 * m + e + 1)[1]:
                        pe.wait_ge(pr_lo_late, low_parts(8 * m + e + 1)[1])
                    for half in range(2):
                        h = p + PAIRS * half
                        for tt in range(HALF):
                            cols = slice(half * FEAT + tt * P, half * FEAT + (tt + 1) * P)
                            dst = av[:, tt * HEADS + h, :]
                            for pt, vt in ((pr_hi, v_hi), (pr_hi, v_lo), (pr_lo, v_hi)):
                                first = e == 0 and half == 0 and tt == 0 and pt is pr_hi and vt is v_hi
                                buf = e % 4 if pt is pr_hi else (8 * m + e) % 3
                                ins = nc.tensor.matmul(dst, pt[buf][:, cols], vt[m % 2][:, st, h, :], start=first,
                                                       stop=(e == 7 and pt is pr_lo), skip_group_check=True)
                    ins.then_inc(av_done, 1)
                if a == plan["att_turn"]:
                    misc_free(("att", m))
                    pe.wait_ge(att_ready, m + 1)
                    for tt in range(HALF):
                        ins = nc.tensor.transpose(misc_ps[:, tt * P:(tt + 1) * P], att[:, tt, :], eye_sb[:, :])
                    ins.then_inc(misc_written, 1)
                if a == plan["x4_turn"]:
                    misc_free(("x4", m))
                    pe.wait_ge(x4_ready, m + 1)
                    for h in range(HALF):
                        ins = nc.tensor.transpose(misc_ps[:, h * P:(h + 1) * P], x4n[:, h * P:(h + 1) * P], eye_sb[:, :])
                    ins.then_inc(misc_written, 1)
                if a == plan["ffn"]:
                    misc_free(("ffn", m))
                    pe.wait_ge(misc_read, misc_no[("x4", m)])
                    for h in range(HALF):
                        ins = nc.tensor.matmul(misc_ps[:, 0:FEAT], x4T[:, h, :], ffn_sb[:, h, :], start=(h == 0), stop=(h == HALF - 1))
                    ins.then_inc(misc_written, 1)

            def wkv(n, w):
                for h in range(HALF):
                    if w == K_TURN + h:
                        if (n, h) != (0, 1):
                            misc_free(("k", n, h))
                        pe.wait_ge(xn_ready, 2 * n + 1)
                        for b in range(BB):
                            ins = nc.tensor.transpose(turn_bank(n, h)[:, b * P:(b + 1) * P], xn[:, b, h * P:(h + 1) * P], eye_sb[:, :])
                        ins.then_inc(misc_written, 1)
                    if w == half_start(n, h) + Y_TURN:
                        misc_free(("y", n, h))
                        pe.wait_ge(yk_ready, 2 * n + h + 1)
                        y = wkv_buffers(n, h)[6]
                        for b in range(BB):
                            ins = nc.tensor.transpose(misc_ps[:, b * P:(b + 1) * P], y[:, b, :], eye_sb[:, :])
                        ins.then_inc(misc_written, 1)
                    if w == X2_TURN + 2 * h:
                        if (n, h) != (0, 1):
                            misc_free(("x2", n, h))
                        pe.wait_ge(xn_ready, 2 * n + 2)
                        for b in range(BB):
                            ins = nc.tensor.transpose(turn_bank(n, h)[:, b * P:(b + 1) * P], xn[:, b, h * P:(h + 1) * P], eye_sb[:, :])
                        ins.then_inc(misc_written, 1)
                if w == GATE:
                    misc_free(("gate", n))
                    pe.wait_ge(gate_w_lo, 1)
                    i = n % 2
                    for b in range(BB):
                        for k in range(HALF):
                            tok = slice(b * P, (b + 1) * P)
                            for xt, wt in ((xT_hi, gw_hi), (xT_lo, gw_hi), (xT_hi, gw_lo)):
                                ins = nc.tensor.matmul(misc_ps[:, b * EXPERTS:(b + 1) * EXPERTS], xt[i][:, k, tok], wt[:, k, :],
                                                       start=(k == 0 and xt is xT_hi and wt is gw_hi),
                                                       stop=(k == HALF - 1 and wt is gw_lo))
                    ins.then_inc(misc_written, 1)
                if w == ROUTE:
                    misc_free(("route", n))
                    pe.wait_ge(route_set, n + 1)
                    for b in range(BB):
                        ins = nc.tensor.transpose(misc_ps[0:EXPERTS, b * P:(b + 1) * P], route[:, b, :], eye_sb[:, :])
                    ins.then_inc(misc_written, 1)

            pe.wait_ge(early_in, 16 * N_EARLY)
            for slot in range(FIRST_SLOT, LAST_SLOT + 1):
                moe_first = slot % 3 in MOE_FIRST["pe"]
                if moe_first:
                    moe(slot)
                for m, a in attn_steps(slot):
                    attention(m, a)
                for n, w in wkv_steps(slot):
                    wkv(n, w)
                if not moe_first:
                    moe(slot)


def kernel(x, ctx_2048, L0_xattn_w, L0_xattn_u, L0_ffn_gate_w, L0_ffn_w13, L0_ffn_w2, L0_ffn_sw13, L0_ffn_sw2,
           L1_ffn_weight, L1_ffn_scale):
    import numpy as np
    import concourse.bacc as bacc
    from concourse.bass_utils import run_bass_kernel_spmd

    def arr(a):
        return np.asarray(a)

    x, c = arr(x), arr(ctx_2048)
    heads = c.reshape(BATCH, 2, PAIRS, CH, FEAT).transpose(0, 1, 3, 2, 4)
    a, b = heads[:, 0], heads[:, 1]
    ctx_heads = np.concatenate([a, a, b, b, a, b], axis=1)

    def rows(shared, routed):
        return np.concatenate([shared, np.zeros((OPEN * P - SHARED, FEAT), shared.dtype), routed.reshape(-1, FEAT)])

    def inner(w):
        return w.reshape(TILES, P, HALF, P).transpose(0, 3, 2, 1)

    w13, sw13 = arr(L0_ffn_w13), arr(L0_ffn_sw13)
    gate = inner(rows(sw13[:SHARED], w13[:, :INNER]))
    up = inner(rows(sw13[SHARED:], w13[:, INNER:]))
    w2 = rows(arr(L0_ffn_sw2).T, arr(L0_ffn_w2).transpose(0, 2, 1)).reshape(TILES, P, FEAT)
    experts = np.concatenate([gate.reshape(TILES, P, FEAT), up.reshape(TILES, P, FEAT), w2], axis=2)

    arrays = {
        "x": x,
        "ctx_feat": c.transpose(0, 2, 1),
        "ctx_heads": ctx_heads,
        "experts": experts,
        "gate_w": arr(L0_ffn_gate_w).T.reshape(HALF, P, EXPERTS).transpose(1, 0, 2),
        "decay_bonus": np.stack([arr(L0_xattn_w), arr(L0_xattn_u)], 1).reshape(HALF, P, 2).transpose(1, 0, 2),
        "ffn_w": arr(L1_ffn_weight).reshape(HALF, P, FEAT).transpose(1, 0, 2),
        "ffn_scale": arr(L1_ffn_scale),
        "eye": np.eye(P, dtype=np.float32),
    }
    arrays = {name: np.ascontiguousarray(v) for name, v in arrays.items()}
    nc = bacc.Bacc("TRN2", target_bir_lowering=False, num_devices=1)
    args = [nc.dram_tensor(name, v.shape, mybir.dt.from_np(v.dtype), kind="ExternalInput").ap() for name, v in arrays.items()]
    out = nc.dram_tensor("out", (BATCH, POS, FEAT), F32, kind="ExternalOutput").ap()
    build(nc, *args, out)
    r = run_bass_kernel_spmd(nc, [arrays], core_ids=[0])
    return r.results[0]["out"]
```
